# Optimizing a Trainium2 kernel written in Bass

```python
import numpy as np
import jax
import jax.numpy as jnp

def _softmax(x, axis=-1):
    return jax.nn.softmax(x, axis=axis)
def _gelu(x):
    return jax.nn.gelu(x, approximate=True)
def _silu(x):
    return jax.nn.silu(x)
def _sigmoid(x):
    return jax.nn.sigmoid(x)
def _layernorm(x, axis=-1, eps=1e-5):
    m = jnp.mean(x, axis=axis, keepdims=True)
    v = jnp.var(x, axis=axis, keepdims=True)
    return (x - m) / jnp.sqrt(v + eps)
def _scatter_add(tgt, idx, src, axis=0):
    return tgt.at[idx].add(src)
def _segment_sum(src, seg, n):
    return jax.ops.segment_sum(src, seg, n)

kernel_name = 'mk_conv_preact_d2_conv_nhwc64_e7ce08'

def setup_inputs(seed: int = 0):
    np.random.seed(seed)
    _w = jnp.asarray
    def _rec_inputs():
        import jax
        import jax.numpy as jnp
        _gk = jax.random.key(seed)
        x = -0.000125 + 0.9999 * jax.random.normal(jax.random.fold_in(_gk, 1), (8, 256, 256, 64), jnp.float32)
        return x
    x = _rec_inputs()
    def _L0_conv_setup():
        import jax, jax.numpy as jnp
        import numpy as np
        MODES = 12
        IN_C = 64
        OUT_C = 64
        key = jax.random.key(seed)
        k1, k2, k3 = jax.random.split(key, 3)
        x = jax.random.normal(k1, (8, 256, 256, IN_C), dtype=jnp.float32)
        w_real = jax.random.normal(k2, (IN_C, OUT_C, MODES, MODES), dtype=jnp.float32) * 0.01
        w_imag = jax.random.normal(k3, (IN_C, OUT_C, MODES, MODES), dtype=jnp.float32) * 0.01
        return {'x': x, 'w_real': w_real, 'w_imag': w_imag}
    _L0_conv_all = _L0_conv_setup()
    _L0_conv_in = {k: v for k, v in _L0_conv_all.items() if k in ('w_real', 'w_imag', )}
    del _L0_conv_all

    def _L1_conv_setup():
        import jax, jax.numpy as jnp
        import numpy as np
        M0F, M0B, M1 = (16, 16, 17)
        key = jax.random.key(seed)
        k1, k2, k3 = jax.random.split(key, 3)
        X = jax.random.normal(k1, (16, 128, 128, 64), dtype=jnp.float32)
        kernel_re = jax.random.uniform(k2, (32, 17, 64, 64), dtype=jnp.float32)
        kernel_im = jax.random.uniform(k3, (32, 17, 64, 64), dtype=jnp.float32)
        return {'X': X, 'kernel_re': kernel_re, 'kernel_im': kernel_im}
    _L1_conv_all = _L1_conv_setup()
    _L1_conv_in = {k: v for k, v in _L1_conv_all.items() if k in ('kernel_re', 'kernel_im', )}
    del _L1_conv_all

    return {
        "x": x,
        "L0_conv_w_real": _L0_conv_in["w_real"],
        "L0_conv_w_imag": _L0_conv_in["w_imag"],
        "L1_conv_kernel_re": _L1_conv_in["kernel_re"],
        "L1_conv_kernel_im": _L1_conv_in["kernel_im"],
    }

def reference(x, L0_conv_w_real, L0_conv_w_imag, L1_conv_kernel_re, L1_conv_kernel_im):
    import jax
    import jax.numpy as jnp
    def _L0_conv_ref(x, w_real, w_imag):
        import jax, jax.numpy as jnp
        import numpy as np
        MODES = 12
        IN_C = 64
        OUT_C = 64
        xc = jnp.transpose(x, (0, 3, 1, 2)).astype(jnp.complex64)
        x_ft = jnp.fft.fft2(xc, axes=(-2, -1))
        x_ft = x_ft[:, :, :MODES, :MODES]
        w = w_real + 1j * w_imag
        out_ft = jnp.einsum('bcmn,comn->bomn', x_ft, w)
        B = x.shape[0]
        H, W = (x.shape[1], x.shape[2])
        out_full = jnp.zeros((B, OUT_C, H, W), dtype=jnp.complex64)
        out_full = out_full.at[:, :, :MODES, :MODES].set(out_ft)
        out = jnp.fft.ifft2(out_full, axes=(-2, -1))
        return jnp.transpose(jnp.real(out), (0, 2, 3, 1))

    def _L1_conv_ref(X, kernel_re, kernel_im):
        import jax, jax.numpy as jnp
        import numpy as np
        M0F, M0B, M1 = (16, 16, 17)
        kernel = kernel_re + 1j * kernel_im
        Co = kernel.shape[-2]
        s1, s2 = (X.shape[-3], X.shape[-2])
        Xf = jnp.fft.rfftn(X, axes=(-3, -2), norm='forward')
        Yf = jnp.zeros(Xf.shape[:-1] + (Co,), dtype=Xf.dtype)
        Yf = Yf.at[:, :M0F, :M1].set(jnp.einsum('xyij,bxyj->bxyi', kernel[:M0F, :M1], Xf[:, :M0F, :M1]))
        Yf = Yf.at[:, -M0B:, :M1].set(jnp.einsum('xyij,bxyj->bxyi', kernel[-M0B:, :M1], Xf[:, -M0B:, :M1]))
        return jnp.fft.irfftn(Yf, axes=(-3, -2), s=(s1, s2), norm='forward')

    def _gn(v, G=32, eps=1e-5):
        B_, H_, W_, C_ = v.shape
        g = v.reshape(B_, H_, W_, G, C_ // G)
        m = jnp.mean(g, axis=(1, 2, 4), keepdims=True)
        s = jnp.var(g, axis=(1, 2, 4), keepdims=True)
        return ((g - m) / jnp.sqrt(s + eps)).reshape(v.shape)

    def _ln_c(v, eps=1e-6):
        m = jnp.mean(v, axis=-1, keepdims=True)
        s = jnp.var(v, axis=-1, keepdims=True)
        return (v - m) / jnp.sqrt(s + eps)

    def _ln_t(v, eps=1e-5):
        m = jnp.mean(v, axis=-1, keepdims=True)
        s = jnp.var(v, axis=-1, keepdims=True)
        return (v - m) / jnp.sqrt(s + eps)

    def _to_tokens(v):
        B_, H_, W_, C_ = v.shape
        return v.reshape(B_, H_ * W_, C_)
    def _from_tokens(t, like):
        return t.reshape(like.shape)

    x = x + _L0_conv_ref(_gn(x), L0_conv_w_real, L0_conv_w_imag)
    x = x + _L1_conv_ref(_gn(x), L1_conv_kernel_re, L1_conv_kernel_im)
    return x


_drawn_inputs = setup_inputs


def setup_inputs(seed=0):
    import zlib

    import numpy as np

    out = dict(_drawn_inputs(seed))
    spreads = {}
    factors = {'L0_conv_w_real': 4.281, 'L0_conv_w_imag': 4.268}
    for name, (base, spread) in spreads.items():
        noise = np.random.default_rng([zlib.crc32(name.encode()), seed]).standard_normal(out[name].shape)
        drawn = base * np.exp(spread * noise) if base else spread * noise
        out[name] = jnp.asarray(drawn.astype(out[name].dtype))
    for name, factor in factors.items():
        out[name] = (out[name] * factor).astype(out[name].dtype)
    return out
```

```python
from contextlib import ExitStack

import numpy as np

import concourse.bass as bass
from concourse import mybir

F32 = mybir.dt.float32
F32R = mybir.dt.float32r
ALU = mybir.AluOpType
ACT = mybir.ActivationFunctionType
AX = mybir.AxisListType

B, H, W, C = 8, 256, 256, 64
P = 128
HT = H // P
WF, WH = 2, W // 2
M0 = 12
MR, NR = 17, 17
MX = 2 * (MR - 1)
MODES = MX * NR
NPIX = H * W
G = C // 2
EPS = 1e-5

SLOTS = 8
WS = WH // SLOTS
SLOT = HT * WF * WS * C
WT = 8
TILES = WH // WT
HB = 2 * MR
NE, NO = NR // 2 + 1, NR // 2
CG = 4
GROUPS = C // CG
BANK = 512

CHUNK = 16
CHUNKS = MODES // CHUNK
KG = CHUNK // 4
QG = 8
QGROUPS = -(-HB // QG)
PIECES = SLOTS // 2
PW = 2 * WS
ZG = BANK // (WF * PW)
ZGROUPS = C // ZG
FT = SLOTS * HT * WF * 2
PT = FT // PIECES
LOW = 64
SPLIT = LOW + HB

def columns(names_widths):
    at, out = 0, {}
    for name, width in names_widths:
        out[name] = (at, width)
        at += width
    return out, at


EARLY, EARLY_W = columns([("rows", HT * WF * 2 * HB), ("even", 2 * NE), ("odd", 2 * NO), ("turn", P), ("flip", P),
                          ("flipturn", P), ("minus_j", P), ("place_re", P), ("place_im", P), ("place_conj", P),
                          ("pair", P), ("pair_top", P), ("spread", P), ("ones", 1), ("eps", 1), ("minus_n_top", 1),
                          ("two_top", 1)])
STEPS = ["group_sums", "mean0", "meansq_x", "mean0_sq", "var0", "inv0", "dc0", "staged0", "staged0_dc", "y0_a", "y0_b",
         "seed_n0", "seed", "yh", "yh_dc", "cross", "cross_yh", "add_modes", "add_conj", "quad", "dquad", "mean1",
         "var1_part", "mean1_sq", "var1", "inv1", "inv1n", "dc1"]
AFTER = {name: i + 1 for i, name in enumerate(STEPS)}
LATE, LATE_W = columns([("ident", P)])
BACK, BACK_W = columns([("rows_high", HT * P), ("rows_low", HT * P), ("cols_high", W), ("cols_low", W)])


def rounded(a):
    bits = np.asarray(a, np.float32).view(np.uint32).astype(np.uint64)
    return ((bits + 0x7FF + ((bits >> 12) & 1)) & 0xFFFFF000).astype(np.uint32).view(np.float32).astype(np.float64)


def constants():
    early, late = np.zeros((P, EARLY_W)), np.zeros((P, LATE_W))

    def put(t, where, name, value, row=0):
        a, w = where[name]
        value = value.reshape(value.shape[0], -1)
        t[row:row + value.shape[0], a:a + value.shape[1]] = value

    m, n, h = np.arange(MR), np.arange(NR), np.arange(H)
    angle = 2 * np.pi * ((h[:, None] * m[None, :]) % H) / H
    basis = np.stack([np.cos(angle), np.sin(angle)], -1)
    rows = np.zeros((P, HT, WF, 2, MR, 2))
    for ht in range(HT):
        for wf in range(WF):
            for odd in range(2):
                rows[:, ht, wf, odd] = basis[ht * P:(ht + 1) * P] * (-1 if wf and odd else 1)
    put(early, EARLY, "rows", rows)
    put(early, EARLY, "even", basis[:WH, 0::2].transpose(0, 2, 1))
    put(early, EARLY, "odd", basis[:WH, 1::2].transpose(0, 2, 1))
    eye, none = np.eye(C), np.zeros((C, C))
    blocks = {"turn": [[none, -eye], [eye, none]], "flip": [[eye, none], [none, -eye]],
              "flipturn": [[none, eye], [eye, none]], "minus_j": [[none, eye], [-eye, none]]}
    for name, b in blocks.items():
        put(early, EARLY, name, np.block(b).T)
    put(early, EARLY, "place_re", np.hstack([0.5 * eye, none]))
    put(early, EARLY, "place_im", np.hstack([none, 0.5 * eye]))
    put(early, EARLY, "place_conj", np.hstack([none, -0.5 * eye]))
    pair = np.kron(np.eye(G), np.ones((2, 2))) / (2 * NPIX)
    put(early, EARLY, "pair", np.block([[pair, pair], [pair, pair]]))
    put(early, EARLY, "pair_top", np.block([[pair, pair], [none, none]]))
    put(early, EARLY, "spread", np.tile(np.kron(np.eye(G), np.ones((1, 2))), (1, 2)) / (2 * NPIX))
    put(early, EARLY, "ones", np.ones((P, 1)))
    put(early, EARLY, "eps", np.full((P, 1), EPS))
    top = np.repeat([1.0, 0.0], C)[:, None]
    put(early, EARLY, "minus_n_top", -NPIX * top)
    put(early, EARLY, "two_top", 2 * top)
    put(late, LATE, "ident", np.eye(P))
    back = np.zeros((P, BACK_W))
    weight = np.where(n == 0, 1.0, 2.0)[:, None]
    for name, value in (("rows", basis.transpose(1, 2, 0).reshape(HB, H)),
                        ("cols", (basis.transpose(2, 1, 0) * weight).reshape(2 * NR, W))):
        high = rounded(value)
        for row in (0, LOW):
            put(back, BACK, name + "_high", high, row)
            put(back, BACK, name + "_low", rounded(value - high), row)
    return early.astype(np.float32), late.astype(np.float32), back.astype(np.float32)


def spectral_layers(nc, x, w_re, w_im, k_re, k_im, early_c, late_c, back_c, out):
    ctx = ExitStack()
    with ctx:
        def sem(name):
            return ctx.enter_context(nc.semaphore(name))

        place = [1152]

        def sb(name, width, dtype=F32, at=None):
            here = place[0] if at is None else at
            if at is None:
                place[0] += -(-width * 4 // 32) * 32
            return nc.alloc_sbuf_tensor_at(name, [P, width], dtype, offset=here)

        ring = sb("ring", SLOTS * SLOT)
        xm_at = place[0]
        xm = sb("xm", MODES * B)
        qs = sb("qs", C * HB, F32R, at=xm_at)
        arena_at = place[0]
        arena = sb("arena", MODES * 2 * B + 2 * WF * PW * C)
        z = sb("z", 2 * WF * PW * C, F32R, at=arena_at + MODES * 2 * B * 4)
        early = sb("early", EARLY_W)
        late = sb("late", LATE_W)
        back = sb("back", BACK_W, F32R)
        small = sb("small", 16 * B)
        banks = ctx.enter_context(nc.psum_tensor("banks", [P, 8, BANK], F32))

        def const(name, rows=P):
            t, where = (early, EARLY) if name in EARLY else (late, LATE)
            a, w = where[name]
            return t[0:rows, a:a + w]

        def split(name, a=0, w=None):
            at, width = BACK[name]
            return back[0:SPLIT, at + a:at + a + (w or width)]

        xs = ring[:, :].rearrange("p (s ht wf w c) -> p s ht wf w c", s=SLOTS, ht=HT, wf=WF, w=WS)
        xpos = ring[:, :].rearrange("p (hf pos g two) -> p hf g pos two", hf=2, g=G, two=2)
        xmv = xm[:, :].rearrange("p (m n b) -> p m n b", n=NR, b=B)

        def part(a, w, rows=P):
            return arena[0:rows, a:a + w], a + w

        rows_f, at = part(0, C * WH, 2 * HB)
        rows_t, at = part(at, 2 * HB * C)
        cols_f, at = part(at, 2 * MR * NR)
        bn, at = part(at, 2 * G * 6)
        sqa, at = part(at, 2 * G * 2)
        sqb, at = part(at, 2 * G * 2)
        sumsq, at = part(at, B * G)
        assert at <= arena.shape[1]
        rows_f = rows_f.rearrange("k (c w) -> k c w", c=C)
        rows_tv = rows_t.rearrange("w (k c) -> w k c", c=C)
        cols_fv = cols_f.rearrange("p (q m n) -> p q m n", q=2, m=MR)
        bnv = bn.rearrange("p (hf g six) -> p hf g six", hf=2, g=G)
        bns = bn.rearrange("p (hg eo three) -> p hg eo three", eo=2, three=3)
        back_raw = arena[:, arena.shape[1] - BACK_W:]
        assert at <= arena.shape[1] - BACK_W
        sumsqv = sumsq.rearrange("p (b g) -> p b g", b=B)
        L0 = M0 * M0
        w0, at0 = part(0, C * L0)
        xs0, at0x = part(at0, L0 * 2 * B)
        y0, at1 = part(at0x, L0 * 2 * B, C)
        yh, at1 = part(at1, L0 * B)
        tmp, at1 = part(at1, L0 * B)
        w0v = w0.rearrange("p (o f) -> p o f", f=L0)
        xs0v = xs0.rearrange("p (m n v b) -> p m n v b", m=M0, n=M0, v=2)
        xs0f = xs0.rearrange("p (f v b) -> p f v b", v=2, b=B)
        y0v = y0.rearrange("p (m n vb) -> p m n vb", m=M0, n=M0)
        y0f = y0.rearrange("p (f v b) -> p f v b", v=2, b=B)
        res, atr = part(0, MODES * 2 * B, C)
        assert atr <= at0
        raw, at2 = part(at0, 2 * CHUNK * C)
        assert at2 <= at0x
        raw2, at3 = part(at0x, 2 * CHUNK * C)
        kt, at3 = part(at3, 2 * CHUNK * C)
        assert at3 <= at1
        xst, at3 = part(at1, 2 * CHUNK * 2 * B)
        assert at3 <= arena.shape[1]
        rawv = raw.rearrange("p (k g ri e j) -> p k g ri e j", k=2, g=KG, ri=2, e=2)
        raw2v = raw2.rearrange("p (k g e rj) -> p k g e rj", k=2, g=KG, e=2)
        ktv = kt.rearrange("p (k f i) -> p k f i", k=2, f=CHUNK)
        xstv = xst.rearrange("p (k f v b) -> p k f v b", k=2, f=CHUNK, v=2)
        resv = res.rearrange("p (m n v b) -> p m n v b", n=NR, v=2, b=B)
        resf = res.rearrange("p (f vb) -> p f vb", vb=2 * B)
        tb = early[0:C, 0:HB * 2 * NR].rearrange("o (m r q n) -> o m r q n", m=MR, r=2, q=2)
        tbf = early[0:C, 0:HB * 2 * NR].rearrange("o (k nb) -> o k nb", k=HB)
        qsv = qs[:, :].rearrange("nb (o k) -> nb o k", k=HB)
        zv = z[:, :].rearrange("p (j wf w o) -> p j wf w o", j=2, wf=WF, w=PW)
        zg_view = z[:, :].rearrange("p (j x o) -> p j o x", j=2, o=C)

        def vec(i, rows=P):
            return small[0:rows, i * B:(i + 1) * B]

        gsum, mean0, mean0_sq, var0, std0, inv0, dc0, quad, dquad = (vec(i) for i in range(9))
        mean1, mean1_sq, var1, std1, inv1, inv1n, meansq_x = (vec(i) for i in range(9, 16))

        consts_loaded, back_loaded = sem("consts_loaded"), sem("back_loaded")
        pads_cleared = sem("pads_cleared")
        x_loaded = [sem(f"x_loaded{s}") for s in range(SLOTS)]
        rows_done, rows_stored = sem("rows_done"), sem("rows_stored")
        turned, turn_stored = sem("turned"), sem("turn_stored")
        cols_done, cols_stored = sem("cols_done"), sem("cols_stored")
        modes_done, modes_stored = sem("modes_done"), sem("modes_stored")
        stats_done, stat_step, sumsq_done = sem("stats_done"), sem("stat_step"), sem("sumsq_done")
        w0_loaded = sem("w0_loaded")
        pe_mix, act_mix, dve_mix = sem("pe_mix"), sem("act_mix"), sem("dve_mix")
        y0_done, y0_stored = sem("y0_done"), sem("y0_stored")
        res_cleared = sem("res_cleared")
        k_loaded = [sem(f"k_loaded{i}") for i in range(2)]
        regrouped_act, regrouped_dve = sem("regrouped_act"), sem("regrouped_dve")
        kt_done, kt_act, kt_dve = sem("kt_done"), sem("kt_act"), sem("kt_dve")
        staged, turned_done, turned_stored = sem("staged"), sem("turned_done"), sem("turned_stored")
        mixed, summed = sem("mixed"), sem("summed")
        split_ready, tb_cleared, tb_minus = sem("split_ready"), sem("tb_cleared"), sem("tb_minus")
        tb_ready, q_done, q_high, q_low = sem("tb_ready"), sem("q_done"), sem("q_high"), sem("q_low")
        z_done, z_high, z_low = sem("z_done"), sem("z_high"), sem("z_low")
        field_done, added = sem("field_done"), sem("added")
        stored = [sem(f"stored{s}") for s in range(SLOTS)]

        x_dram = x.rearrange("b (ht p) (wf s w) c -> b s ht p wf (w c)", p=P, wf=WF, s=SLOTS)
        out_dram = out.rearrange("b (ht p) (wf s w) c -> b s ht p wf (w c)", p=P, wf=WF, s=SLOTS)
        k_dram = [k.rearrange("x y i j -> (x y i j)").rearrange("(k g p ej) -> k p g ej", g=KG, p=P, ej=2 * C)
                  for k in (k_re, k_im)]

        block = ctx.enter_context(nc.Block())

        @block.sync
        def _(sp):
            sp.dma_start(early[:, :], early_c).then_inc(consts_loaded, 16)
            sp.dma_start(late[:, :], late_c).then_inc(consts_loaded, 16)
            sp.dma_start(back_raw, back_c).then_inc(back_loaded, 16)

            def load_x(b, s):
                for ht in range(HT):
                    src = x_dram[bass.ds(b, 1), s, ht].rearrange("b p wf n -> p (b wf) n")
                    sp.dma_start(xs[:, s, ht].rearrange("p wf w c -> p wf (w c)"), src).then_inc(x_loaded[s], 16)

            for s in range(SLOTS):
                load_x(0, s)
            with sp.Fori(1, B) as b:
                for s in range(SLOTS):
                    sp.wait_ge(rows_done, (b - 1) * TILES + 2 * s + 2)
                    if s % 4 == 0:
                        sp.wait_ge(stats_done, (b - 1) * TILES + 2 * s + 2)
                    load_x(b, s)
            sp.wait_ge(cols_done, B)
            sp.wait_ge(turned, B * GROUPS)
            sp.dma_start(w0v[0:C], w_re.rearrange("c o m n -> c o (m n)")).then_inc(w0_loaded, 16)
            sp.dma_start(w0v[C:P], w_im.rearrange("c o m n -> c o (m n)")).then_inc(w0_loaded, 16)

            def load_k(k, i):
                for ri in range(2):
                    src = k_dram[ri][k] if isinstance(k, int) else \
                        k_dram[ri][bass.ds(k, 1)].rearrange("k p g ej -> p (k g) ej")
                    sp.dma_start(rawv[:, i, :, ri].rearrange("p g e j -> p g (e j)"), src).then_inc(k_loaded[i], 16)

            sp.wait_ge(y0_done, 5)
            load_k(0, 0)
            load_k(1, 1)
            with sp.Fori(1, CHUNKS // 2) as kk:
                for i in range(2):
                    sp.wait_ge(regrouped_act, (kk - 1) * 2 + i + 1)
                    sp.wait_ge(regrouped_dve, (kk - 1) * 2 + i + 1)
                    load_k(2 * kk + i, i)

            def write_out(b, s, k):
                sp.wait_ge(added, k * FT + (s + 1) * (FT // SLOTS))
                for ht in range(HT):
                    dst = out_dram[bass.ds(b, 1), s, ht].rearrange("b p wf n -> p (b wf) n")
                    sp.dma_start(dst, xs[:, s, ht].rearrange("p wf w c -> p wf (w c)")).then_inc(stored[s], 16)

            def image(k, b, again):
                for s in range(SLOTS):
                    write_out(b, s, k)
                    if again and s >= 2:
                        sp.wait_ge(stored[s - 2], k * 32 + 32)
                        load_x(k, s - 2)
                if again:
                    for s in (SLOTS - 2, SLOTS - 1):
                        sp.wait_ge(stored[s], k * 32 + 32)
                        load_x(k, s)

            image(0, B - 1, True)
            with sp.Fori(1, B - 1) as k:
                image(k, k - 1, True)
            image(B - 1, B - 2, False)
            for s in range(SLOTS):
                sp.wait_ge(stored[s], B * 32)

        @block.tensor
        def _(pe):
            row_basis = const("rows").rearrange("p (ht wf k) -> p ht wf k", ht=HT, wf=WF)

            def row_product(b, t, i):
                ht, wf = i // WF, i % WF
                if i == 0:
                    pe.wait_ge(x_loaded[t // 2], b * 32 + 32)
                    if not (isinstance(b, int) and b == 0 and t < 4):
                        pe.wait_ge(rows_stored, b * TILES + t - 3)
                last = nc.tensor.matmul(banks[0:2 * HB, t % 4], row_basis[:, ht, wf],
                                        xs[:, t // 2, ht, wf, (t % 2) * WT:(t % 2 + 1) * WT, :],
                                        start=(i == 0), stop=(i == HT * WF - 1))
                if i == HT * WF - 1:
                    last.then_inc(rows_done, 1)

            def turn_group(b, g, first):
                if g == 0:
                    pe.wait_ge(rows_stored, b * TILES + TILES)
                if not first:
                    pe.wait_ge(turn_stored, b * GROUPS + g - 1)
                    if g < 2:
                        pe.wait_ge(modes_stored, b * 2)
                elif g >= 2:
                    pe.wait_ge(turn_stored, g - 1)
                for j in range(CG):
                    last = nc.tensor.transpose(banks[:, 4 + g % 2, j * 2 * HB:(j + 1) * 2 * HB],
                                               rows_f[:, g * CG + j, :], const("ident")[0:2 * HB, 0:2 * HB])
                last.then_inc(turned, 1)

            def column_mode(b, i, first):
                if i == 0:
                    pe.wait_ge(turn_stored, b * GROUPS + GROUPS)
                    if not first:
                        pe.wait_ge(cols_stored, b * 2)
                odd, m = i // MR, i % MR
                name, width = (("even", 2 * NE), ("odd", 2 * NO))[odd]
                last = nc.tensor.matmul(banks[:, 6 + odd, m * width:(m + 1) * width],
                                        rows_t[:, i * 2 * C:(i + 1) * 2 * C], const(name), start=True, stop=True)
                if i == 2 * MR - 1:
                    last.then_inc(cols_done, 1)

            def complex_modes(b):
                pe.wait_ge(cols_stored, b * 2 + 2)
                for minus, mats in ((0, ("ident", "turn")), (1, ("flip", "flipturn"))):
                    for q in range(2):
                        src = cols_fv[:, q, 16:0:-1, :] if minus else cols_fv[:, q, 0:16, :]
                        last = nc.tensor.matmul(banks[:, 4 + minus, 0:MODES // 2], const(mats[q]), src,
                                                start=(q == 0), stop=(q == 1))
                    last.then_inc(modes_done, 1)

            pe.wait_ge(consts_loaded, 32)
            for t in range(TILES):
                for i in range(4):
                    row_product(0, t, i)

            def forward(b, first):
                for t in range(4):
                    for i in range(4):
                        row_product(b, t, i)
                        turn_group(b - 1, t * 4 + i, first)
                ahead = 2 * MR - 7 * 4
                for i in range(ahead):
                    column_mode(b - 1, i, first)
                for t in range(4, TILES):
                    for i in range(4):
                        row_product(b, t, i)
                        if t < 11:
                            column_mode(b - 1, ahead + (t - 4) * 4 + i, first)
                    if t == 12:
                        complex_modes(b - 1)

            forward(1, True)
            with pe.Fori(2, B) as b:
                forward(b, False)
            for g in range(GROUPS):
                turn_group(B - 1, g, False)
            for i in range(2 * MR):
                column_mode(B - 1, i, False)
            complex_modes(B - 1)

            pe.wait_ge(sumsq_done, B)
            pe.wait_ge(cols_stored, 2 * B)
            for b in range(B):
                last = nc.tensor.matmul(banks[0:G, 6, b:b + 1], sumsqv[:, b, :], const("ones"), start=True, stop=True)
            last.then_inc(pe_mix, 1)
            pe.wait_ge(modes_stored, 2 * B)
            nc.tensor.matmul(banks[:, 7, 0:B], const("pair_top"), xm[:, 0:B], start=True, stop=True)
            pe.wait_ge(dve_mix, AFTER["group_sums"])
            nc.tensor.matmul(banks[:, 7, B:2 * B], const("spread", G), gsum[0:G], start=True, stop=True
                             ).then_inc(pe_mix, 1)
            pe.wait_ge(dve_mix, AFTER["staged0_dc"])
            for t in range(3):
                nc.tensor.matmul(banks[:, t, 0:48 * B], const("minus_j"), xs0f[:, t * 48:(t + 1) * 48, 0, :],
                                 start=True, stop=True).then_inc(pe_mix, 1)
            pe.wait_ge(w0_loaded, 32)
            for f in range(L0):
                if f % 48 == 0:
                    pe.wait_ge(act_mix, 2 + f // 48)
                last = nc.tensor.matmul(banks[0:C, 3 + f // 32, (f % 32) * 2 * B:(f % 32 + 1) * 2 * B],
                                        w0v[:, :, f], xs0f[:, f], start=True, stop=True)
                if f % 32 == 31 or f == L0 - 1:
                    last.then_inc(y0_done, 1)
            pe.wait_ge(y0_stored, 3)
            pe.wait_ge(dve_mix, AFTER["y0_b"])
            for t in range(3):
                for v, name in enumerate(("place_re", "place_im")):
                    nc.tensor.matmul(banks[:, t, 0:48 * B], const(name, C), y0f[:, t * 48:(t + 1) * 48, v, :],
                                     start=(v == 0), stop=(v == 1))
            for v, name in enumerate(("place_re", "place_conj")):
                last = nc.tensor.matmul(banks[:, 3, 0:(M0 - 1) * B], const(name, C),
                                        y0v[:, M0 - 1:0:-1, 0, v * B:(v + 1) * B], start=(v == 0), stop=(v == 1))
            last.then_inc(pe_mix, 1)
            pe.wait_ge(dve_mix, AFTER["dquad"])
            nc.tensor.matmul(banks[:, 4, 0:B], const("pair_top"), xm[:, 0:B], start=True, stop=True)
            nc.tensor.matmul(banks[:, 4, B:2 * B], const("pair"), dquad, start=True, stop=True).then_inc(pe_mix, 1)

            def prepare(k, i, reused):
                pe.wait_ge(regrouped_act, k + 1)
                pe.wait_ge(regrouped_dve, k + 1)
                if reused:
                    pe.wait_ge(kt_act, k - 1)
                    pe.wait_ge(kt_dve, k - 1)
                for e in range(2):
                    for g in range(KG):
                        last = nc.tensor.transpose(banks[:, 2 * i + e, g * P:(g + 1) * P], raw2v[:, i, g, e, :],
                                                   const("ident"))
                    last.then_inc(kt_done, 1)
                pe.wait_ge(staged, k + 1)
                if reused:
                    pe.wait_ge(turned_stored, k - 1)
                nc.tensor.matmul(banks[:, 4 + i, 0:CHUNK * B], const("minus_j"), xstv[:, i, :, 0, :],
                                 start=True, stop=True).then_inc(turned_done, 1)

            def mix(k, i, reused):
                pe.wait_ge(kt_act, k + 1)
                pe.wait_ge(kt_dve, k + 1)
                pe.wait_ge(turned_stored, k + 1)
                if reused:
                    pe.wait_ge(summed, k - 1)
                for f in range(CHUNK):
                    last = nc.tensor.matmul(banks[0:C, 6 + i, f * 2 * B:(f + 1) * 2 * B], ktv[:, i, f], xstv[:, i, f],
                                            start=True, stop=True)
                last.then_inc(mixed, 1)

            prepare(0, 0, False)
            prepare(1, 1, False)
            mix(0, 0, False)
            prepare(2, 0, True)
            mix(1, 1, False)
            with pe.Fori(1, CHUNKS // 2 - 1) as kk:
                prepare(2 * kk + 1, 1, True)
                mix(2 * kk, 0, True)
                prepare(2 * kk + 2, 0, True)
                mix(2 * kk + 1, 1, True)
            prepare(CHUNKS - 1, 1, True)
            mix(CHUNKS - 2, 0, True)
            mix(CHUNKS - 1, 1, True)

            def inverse(k, first):
                pe.wait_ge(tb_ready, k + 1)
                for j in range(QGROUPS):
                    if not (first and j < 2):
                        pe.wait_ge(q_low, k * QGROUPS + j - 1)
                    a = j * QG * 2 * NR
                    last = nc.tensor.matmul(banks[:, j % 2, 0:C], early[0:C, a:a + P], const("ident")[0:C, 0:C],
                                            start=True, stop=True)
                    for c in range(1, min(QG, HB - j * QG)):
                        last = nc.tensor.transpose(banks[0:2 * NR, j % 2, c * C:(c + 1) * C], tbf[:, j * QG + c, :],
                                                   const("ident")[0:C, 0:C])
                    last.then_inc(q_done, 1)
                pe.wait_ge(q_low, k * QGROUPS + QGROUPS)
                if first:
                    pe.wait_ge(pads_cleared, 2)
                    pe.wait_ge(split_ready, 1)

                def columns_piece(j):
                    for zg in range(ZGROUPS):
                        n = j * ZGROUPS + zg
                        if not (first and n < 2):
                            pe.wait_ge(z_low, k * PIECES * ZGROUPS + n - 1)
                        for c in range(ZG):
                            for part in ("high", "low"):
                                where = split("cols_" + part).rearrange("nb (wf w) -> nb wf w", wf=WF)
                                last = nc.tensor.matmul(banks[0:HB, 2 + zg % 2, c * WF * PW:(c + 1) * WF * PW],
                                                        qsv[0:SPLIT, zg * ZG + c, :], where[:, :, j * PW:(j + 1) * PW],
                                                        start=(part == "high"), stop=(part == "low"))
                        last.then_inc(z_done, 1)

                def rows_piece(j):
                    pe.wait_ge(z_low, k * PIECES * ZGROUPS + (j + 1) * ZGROUPS)
                    for t in range(j * PT, (j + 1) * PT):
                        s, ht, wf, wh = t // 8, t // 4 % 2, t // 2 % 2, t % 2
                        if not (first and t < 4):
                            pe.wait_ge(added, k * FT + t - 3)
                        w_at = s % 2 * WS + wh * WT
                        for part in ("high", "low"):
                            last = nc.tensor.matmul(banks[:, 4 + t % 4, :], split("rows_" + part, ht * P, P),
                                                    zv[0:SPLIT, j % 2, wf, w_at:w_at + WT, :],
                                                    start=(part == "high"), stop=(part == "low"))
                        last.then_inc(field_done, 1)

                columns_piece(0)
                for j in range(PIECES):
                    if j + 1 < PIECES:
                        columns_piece(j + 1)
                    rows_piece(j)

            inverse(0, True)
            with pe.Fori(1, B) as k:
                inverse(k, False)

        @block.scalar
        def _(act):
            def store_rows(b, t, reused):
                act.wait_ge(rows_done, b * TILES + t + 1)
                if reused and t == 0:
                    act.wait_ge(turned, b * GROUPS)
                nc.scalar.copy(rows_f[:, :, t * WT:(t + 1) * WT].rearrange("k c w -> k w c"),
                               banks[0:2 * HB, t % 4, :].rearrange("k (w c) -> k w c", c=C)).then_inc(rows_stored, 1)

            def store_turned(b, g, reused):
                act.wait_ge(turned, b * GROUPS + g + 1)
                if reused and g == 0:
                    act.wait_ge(cols_done, b)
                nc.scalar.copy(rows_tv[:, :, g * CG:(g + 1) * CG].rearrange("w k c -> w c k"),
                               banks[:, 4 + g % 2, 0:CG * 2 * HB].rearrange("w (c k) -> w c k", c=CG)
                               ).then_inc(turn_stored, 1)

            def store_columns(b, reused):
                act.wait_ge(cols_done, b + 1)
                if reused:
                    act.wait_ge(modes_done, 2 * b)
                for odd, n in ((0, NE), (1, NO)):
                    nc.scalar.copy(cols_fv[:, :, :, odd::2].rearrange("p q m n -> p m q n"),
                                   banks[:, 6 + odd, 0:MR * 2 * n].rearrange("p (m q n) -> p m q n", m=MR, q=2)
                                   ).then_inc(cols_stored, 1)

            def store_modes(b):
                act.wait_ge(modes_done, 2 * b + 2)
                for minus in range(2):
                    dst = xm[:, :].rearrange("p (f b) -> p f b", b=B)[:, minus * MODES // 2:(minus + 1) * MODES // 2,
                                                                     bass.ds(b, 1)]
                    nc.scalar.copy(dst, banks[:, 4 + minus, 0:MODES // 2].rearrange("p (f b) -> p f b", b=1)
                                   ).then_inc(modes_stored, 1)

            act.wait_ge(back_loaded, 16)
            nc.scalar.copy(back[:, :], back_raw).then_inc(split_ready, 1)
            for t in range(TILES):
                store_rows(0, t, False)

            def forward(b, first):
                for g in range(GROUPS):
                    store_turned(b - 1, g, not first)
                for t in range(11):
                    store_rows(b, t, True)
                store_columns(b - 1, not first)
                for t in range(11, 13):
                    store_rows(b, t, True)
                store_modes(b - 1)
                for t in range(13, TILES):
                    store_rows(b, t, True)

            forward(1, True)
            with act.Fori(2, B) as b:
                forward(b, False)
            for g in range(GROUPS):
                store_turned(B - 1, g, True)
            store_columns(B - 1, True)
            store_modes(B - 1)

            act.wait_ge(dve_mix, AFTER["var0"])
            nc.scalar.activation(std0, var0, ACT.Sqrt, bias=const("eps")).then_inc(act_mix, 1)
            for t in range(3):
                act.wait_ge(pe_mix, 3 + t)
                nc.scalar.copy(xs0f[:, t * 48:(t + 1) * 48, 1, :],
                               banks[:, t, 0:48 * B].rearrange("p (f b) -> p f b", b=B)).then_inc(act_mix, 1)
            for t, n in ((0, 32), (2, 32), (4, 16)):
                act.wait_ge(y0_done, t + 1)
                nc.scalar.copy(y0[:, t * BANK:t * BANK + n * 2 * B], banks[0:C, 3 + t, 0:n * 2 * B]
                               ).then_inc(y0_stored, 1)
            act.wait_ge(dve_mix, AFTER["var1"])
            nc.scalar.activation(std1, var1, ACT.Sqrt, bias=const("eps")).then_inc(act_mix, 1)

            def regroup(k, i, loads, reused):
                act.wait_ge(k_loaded[i], loads * 32)
                if reused:
                    act.wait_ge(kt_done, 2 * k - 2)
                nc.scalar.copy(raw2v[:, i, :, :, 0:C], rawv[:, i, :, 0]).then_inc(regrouped_act, 1)

            def prepare(k, i, reused):
                act.wait_ge(kt_done, 2 * k + 1)
                if reused:
                    act.wait_ge(mixed, k - 1)
                nc.scalar.copy(ktv[:, i, :, 0::2], banks[:, 2 * i, :].rearrange("p (f i) -> p f i", f=CHUNK)
                               ).then_inc(kt_act, 1)
                act.wait_ge(turned_done, k + 1)
                nc.scalar.copy(xstv[:, i, :, 1, :], banks[:, 4 + i, 0:CHUNK * B].rearrange("p (f b) -> p f b", b=B)
                               ).then_inc(turned_stored, 1)

            act.wait_ge(pe_mix, 6)
            act.wait_ge(dve_mix, AFTER["dquad"])
            regroup(0, 0, 1, False)
            regroup(1, 1, 1, False)
            prepare(0, 0, False)
            regroup(2, 0, 2, True)
            prepare(1, 1, False)
            with act.Fori(1, CHUNKS // 2 - 1) as kk:
                regroup(2 * kk + 1, 1, kk + 1, True)
                prepare(2 * kk, 0, True)
                regroup(2 * kk + 2, 0, kk + 2, True)
                prepare(2 * kk + 1, 1, True)
            regroup(CHUNKS - 1, 1, CHUNKS // 2, True)
            prepare(CHUNKS - 2, 0, True)
            prepare(CHUNKS - 1, 1, True)

            def inverse(k):
                for j in range(QGROUPS):
                    n = min(QG, HB - j * QG)
                    act.wait_ge(q_done, k * QGROUPS + j + 1)
                    nc.scalar.copy(qsv[0:2 * NR, :, j * QG:j * QG + n].rearrange("nb o k -> nb k o"),
                                   banks[0:2 * NR, j % 2, 0:n * C].rearrange("nb (k o) -> nb k o", o=C)
                                   ).then_inc(q_high, 1)
                for n in range(PIECES * ZGROUPS):
                    j, zg = n // ZGROUPS, n % ZGROUPS
                    act.wait_ge(z_done, k * PIECES * ZGROUPS + n + 1)
                    nc.scalar.copy(zg_view[0:HB, j % 2, zg * ZG:(zg + 1) * ZG, :],
                                   banks[0:HB, 2 + zg % 2, :].rearrange("p (o x) -> p o x", o=ZG)
                                   ).then_inc(z_high, 1)

            act.wait_ge(pads_cleared, 2)
            inverse(0)
            with act.Fori(1, B) as k:
                inverse(k)

        @block.gpsimd
        def _(pool):
            pool.wait_ge(y0_done, 5)
            nc.gpsimd.memset(res, 0.0).then_inc(res_cleared, 1)
            pool.wait_ge(staged, CHUNKS)
            nc.gpsimd.memset(qs[:, :].bitcast(F32), 0.0).then_inc(pads_cleared, 1)
            pool.wait_ge(summed, CHUNKS)
            nc.gpsimd.memset(z[:, :].bitcast(F32), 0.0).then_inc(pads_cleared, 1)

        @block.vector
        def _(dve):
            def statistics(b):
                for hf in range(2):
                    for s in range(4 * hf, 4 * hf + 4):
                        dve.wait_ge(x_loaded[s], b * 32 + 32)
                    for g in range(G):
                        last = nc.vector.bn_stats(bnv[:, hf, g, :], xpos[:, hf, g])
                    last.then_inc(stats_done, TILES // 2)
                dve.wait_ge(stats_done, b * TILES + TILES)
                nc.vector.tensor_tensor(sqa.rearrange("p (x y) -> p x y", y=2), bns[:, :, :, 1], bns[:, :, :, 1],
                                        ALU.mult).then_inc(stat_step, 1)
                dve.wait_ge(stat_step, 2 * b + 1)
                nc.vector.scalar_tensor_tensor(sqb.rearrange("p (x y) -> p x y", y=2),
                                               sqa.rearrange("p (x y) -> p x y", y=2), float(SLOTS // 2 * SLOT // C),
                                               bns[:, :, :, 2], ALU.mult, ALU.add).then_inc(stat_step, 1)
                dve.wait_ge(stat_step, 2 * b + 2)
                nc.vector.tensor_reduce(sumsqv[:, bass.ds(b, 1), :].rearrange("p b g -> p (b g)"),
                                        sqb.rearrange("p (hf g eo) -> p g hf eo", hf=2, g=G), AX.XY,
                                        ALU.add).then_inc(sumsq_done, 1)

            with dve.Fori(0, B) as b:
                statistics(b)

            done = [0]

            def step(name, ins):
                done[0] += 1
                assert AFTER[name] == done[0]
                ins.then_inc(dve_mix, 1)

            def after(name):
                dve.wait_ge(dve_mix, AFTER[name])

            v = nc.vector
            dve.wait_ge(pe_mix, 1)
            step("group_sums", v.tensor_copy(gsum[0:G], banks[0:G, 6, 0:B]))
            dve.wait_ge(pe_mix, 2)
            step("mean0", v.tensor_copy(mean0, banks[:, 7, 0:B]))
            step("meansq_x", v.tensor_copy(meansq_x, banks[:, 7, B:2 * B]))
            after("meansq_x")
            step("mean0_sq", v.tensor_tensor(mean0_sq, mean0, mean0, ALU.mult))
            after("mean0_sq")
            step("var0", v.tensor_tensor(var0, meansq_x, mean0_sq, ALU.subtract))
            dve.wait_ge(act_mix, 1)
            step("inv0", v.reciprocal(inv0, std0))
            dve.wait_ge(modes_stored, 2 * B)
            step("dc0", v.scalar_tensor_tensor(dc0, mean0, const("minus_n_top"), xm[:, 0:B], ALU.mult, ALU.add))
            after("dc0")
            step("staged0", v.tensor_tensor(xs0v[:, :, :, 0, :], xmv[:, 0:M0, 0:M0, :],
                                            inv0.rearrange("p (m n b) -> p m n b", m=1, n=1
                                                           ).broadcast_to([P, M0, M0, B]), ALU.mult))
            after("staged0")
            step("staged0_dc", v.tensor_tensor(xs0[:, 0:B], dc0, inv0, ALU.mult))
            for t, name in ((1, "y0_a"), (3, "y0_b")):
                dve.wait_ge(y0_done, t + 1)
                step(name, v.tensor_copy(y0[:, t * BANK:(t + 1) * BANK], banks[0:C, 3 + t, :]))
            dve.wait_ge(y0_stored, 3)
            dve.wait_ge(res_cleared, 1)
            after("y0_b")
            resm = res.rearrange("p (m n vb) -> p m n vb", m=MX, n=NR)
            step("seed_n0", v.tensor_scalar(resm[:, 0:M0, 0, :], y0v[:, :, 0, :], 1.0 / NPIX, None, ALU.mult))
            step("seed", v.tensor_scalar(resm[:, 0:M0, 1:M0, :], y0v[:, :, 1:M0, :], 0.5 / NPIX, None, ALU.mult))
            dve.wait_ge(pe_mix, 6)
            step("yh", v.tensor_copy(yh.rearrange("p (t f) -> p t f", t=3), banks[:, 0:3, 0:48 * B]))
            after("yh")
            step("yh_dc", v.tensor_scalar(yh[:, 0:B], banks[:, 0, 0:B], const("two_top"), None, ALU.mult))
            after("yh_dc")
            xsel = xmv[:, 0:M0, 0:M0, :].rearrange("p m n b -> p m (n b)")
            yhm = yh.rearrange("p (m nb) -> p m nb", m=M0)
            step("cross", v.scalar_tensor_tensor(tmp.rearrange("p (m nb) -> p m nb", m=M0), xsel, 2.0, yhm,
                                                 ALU.mult, ALU.add))
            after("cross")
            step("cross_yh", v.tensor_tensor(tmp, tmp, yh, ALU.mult))
            step("add_modes", v.tensor_tensor(xsel, xsel, yhm, ALU.add))
            step("add_conj", v.tensor_tensor(xmv[:, MX - M0 + 1:MX, 0, :], xmv[:, MX - M0 + 1:MX, 0, :],
                                             banks[:, 3, 0:(M0 - 1) * B].rearrange("p (m b) -> p m b", b=B), ALU.add))
            after("add_conj")
            step("quad", v.tensor_reduce(quad, tmp.rearrange("p (f b) -> p b f", b=B), AX.X, ALU.add))
            after("quad")
            step("dquad", v.scalar_tensor_tensor(dquad, quad, 2.0, tmp[:, 0:B], ALU.mult, ALU.subtract))
            dve.wait_ge(pe_mix, 7)
            step("mean1", v.tensor_copy(mean1, banks[:, 4, 0:B]))
            step("var1_part", v.scalar_tensor_tensor(inv1, banks[:, 4, B:2 * B], 1.0 / NPIX, meansq_x, ALU.mult,
                                                     ALU.add))
            after("var1_part")
            step("mean1_sq", v.tensor_tensor(mean1_sq, mean1, mean1, ALU.mult))
            after("mean1_sq")
            step("var1", v.tensor_tensor(var1, inv1, mean1_sq, ALU.subtract))
            dve.wait_ge(act_mix, 5)
            step("inv1", v.reciprocal(inv1, std1))
            after("inv1")
            step("inv1n", v.tensor_scalar(inv1n, inv1, 1.0 / NPIX, None, ALU.mult))
            step("dc1", v.scalar_tensor_tensor(xm[:, 0:B], mean1, const("minus_n_top"), xm[:, 0:B], ALU.mult,
                                               ALU.add))
            after("dc1")

            xf = xm[:, :].rearrange("p (f b) -> p f b", b=B)

            def regroup(k, i, loads, reused):
                dve.wait_ge(k_loaded[i], loads * 32)
                if reused:
                    dve.wait_ge(kt_done, 2 * k - 2)
                v.tensor_copy(raw2v[:, i, :, :, C:2 * C], rawv[:, i, :, 1]).then_inc(regrouped_dve, 1)

            def prepare(k, i, reused):
                if reused:
                    dve.wait_ge(mixed, k - 1)
                v.tensor_tensor(xstv[:, i, :, 0, :], xf[:, bass.ds(k * CHUNK, CHUNK), :],
                                inv1n.rearrange("p (f b) -> p f b", f=1).broadcast_to([P, CHUNK, B]), ALU.mult
                                ).then_inc(staged, 1)
                dve.wait_ge(kt_done, 2 * k + 2)
                v.tensor_copy(ktv[:, i, :, 1::2], banks[:, 2 * i + 1, :].rearrange("p (f i) -> p f i", f=CHUNK)
                              ).then_inc(kt_dve, 1)

            def add_up(k, i):
                dve.wait_ge(mixed, k + 1)
                dst = resf[:, bass.ds(k * CHUNK, CHUNK), :]
                v.tensor_tensor(dst, dst, banks[0:C, 6 + i, 0:CHUNK * 2 * B].rearrange("p (f vb) -> p f vb", f=CHUNK),
                                ALU.add).then_inc(summed, 1)

            regroup(0, 0, 1, False)
            regroup(1, 1, 1, False)
            prepare(0, 0, False)
            regroup(2, 0, 2, True)
            prepare(1, 1, False)
            add_up(0, 0)
            regroup(3, 1, 2, True)
            prepare(2, 0, True)
            add_up(1, 1)
            with dve.Fori(1, CHUNKS // 2 - 1) as kk:
                regroup(2 * kk + 2, 0, kk + 2, True)
                prepare(2 * kk + 1, 1, True)
                add_up(2 * kk, 0)
                regroup(2 * kk + 3, 1, kk + 2, True)
                prepare(2 * kk + 2, 0, True)
                add_up(2 * kk + 1, 1)
            prepare(CHUNKS - 1, 1, True)
            add_up(CHUNKS - 2, 0)
            add_up(CHUNKS - 1, 1)
            dve.wait_ge(summed, CHUNKS)

            v.memset(tb[:, 0, 1], 0.0).then_inc(tb_cleared, 1)
            dve.wait_ge(tb_cleared, 1)

            def bases(k, b):
                plus = resv[:, 1:MR - 1, :, :, bass.ds(b, 1)].rearrange("o m n v b -> o m v (n b)")
                minus = resv[:, MR:MX, :, :, bass.ds(b, 1)].rearrange("o m n v b -> o m v (n b)")
                edge = resv[:, 0:MR:MR - 1, :, :, bass.ds(b, 1)].rearrange("o m n v b -> o m v (n b)")
                inner, back = tb[:, 1:MR - 1], tb[:, MR - 2:0:-1]
                v.tensor_copy(back[:, :, 0], minus)
                v.tensor_scalar(back[:, :, 1, 0], minus[:, :, 1], -1.0, None, ALU.mult)
                v.tensor_copy(back[:, :, 1, 1], minus[:, :, 0]).then_inc(tb_minus, 1)
                v.tensor_copy(tb[:, 0:MR:MR - 1, 0], edge)
                v.tensor_scalar(tb[:, MR - 1, 1, 0], edge[:, 1, 1], -1.0, None, ALU.mult)
                v.tensor_copy(tb[:, MR - 1, 1, 1], edge[:, 1, 0])
                dve.wait_ge(tb_minus, k + 1)
                v.tensor_tensor(inner[:, :, 0], inner[:, :, 0], plus, ALU.add)
                v.tensor_tensor(inner[:, :, 1, 0], inner[:, :, 1, 0], plus[:, :, 1], ALU.add)
                v.tensor_tensor(inner[:, :, 1, 1], inner[:, :, 1, 1], plus[:, :, 0], ALU.subtract
                                ).then_inc(tb_ready, 1)

            def low_columns(k):
                for j in range(QGROUPS):
                    n = min(QG, HB - j * QG)
                    dve.wait_ge(q_high, k * QGROUPS + j + 1)
                    part = qsv[:, :, j * QG:j * QG + n].rearrange("nb o k -> nb k o")
                    v.tensor_tensor(part[LOW:LOW + 2 * NR], banks[0:2 * NR, j % 2, 0:n * C].rearrange(
                        "nb (k o) -> nb k o", o=C), part[0:2 * NR].bitcast(F32), ALU.subtract).then_inc(q_low, 1)

            def image(k, more):
                def low_parts(j):
                    for zg in range(ZGROUPS):
                        dve.wait_ge(z_high, k * PIECES * ZGROUPS + j * ZGROUPS + zg + 1)
                        part = zg_view[:, j % 2, zg * ZG:(zg + 1) * ZG, :]
                        v.tensor_tensor(part[LOW:SPLIT], banks[0:HB, 2 + zg % 2, :].rearrange("p (o x) -> p o x", o=ZG),
                                        part[0:HB].bitcast(F32), ALU.subtract).then_inc(z_low, 1)

                low_columns(k)
                low_parts(0)
                for j in range(PIECES):
                    if j + 1 < PIECES:
                        low_parts(j + 1)
                    elif more:
                        dve.wait_ge(q_done, k * QGROUPS + QGROUPS)
                        bases(k + 1, k)
                    for t in range(j * PT, (j + 1) * PT):
                        s, ht, wf, wh = t // 8, t // 4 % 2, t // 2 % 2, t % 2
                        if t % 8 == 0:
                            dve.wait_ge(x_loaded[s], k * 32 + B * 32)
                        dve.wait_ge(field_done, k * FT + t + 1)
                        dst = xs[:, s, ht, wf, wh * WT:(wh + 1) * WT, :]
                        v.tensor_tensor(dst, dst, banks[:, 4 + t % 4, :].rearrange("p (w c) -> p w c", c=C),
                                        ALU.add).then_inc(added, 1)

            bases(0, B - 1)
            image(0, True)
            with dve.Fori(1, B - 1) as k:
                image(k, True)
            image(B - 1, False)


_INS = ["x", "L0_conv_w_real", "L0_conv_w_imag", "L1_conv_kernel_re", "L1_conv_kernel_im"]


def kernel(**inputs):
    import numpy as _np
    import concourse.bacc as _bacc
    from concourse import mybir as _mybir
    from concourse.bass_utils import run_bass_kernel_spmd as _run

    nc = _bacc.Bacc("TRN2", target_bir_lowering=False, num_devices=1, dynamic_dma_scratch_size=1024)
    early_c, late_c, back_c = constants()
    arrays = {name: _np.ascontiguousarray(inputs[name]) for name in _INS}
    arrays["early_c"], arrays["late_c"], arrays["back_c"] = early_c, late_c, back_c
    args = [nc.dram_tensor(f"in_{n}", a.shape, _mybir.dt.from_np(a.dtype), kind="ExternalInput").ap()
            for n, a in arrays.items()]
    out = nc.dram_tensor("out_0", (B, H, W, C), _mybir.dt.float32, kind="ExternalOutput").ap()
    spectral_layers(nc, *args, out)
    r = _run(nc, [{f"in_{n}": a for n, a in arrays.items()}], core_ids=[0])
    return r.results[0]["out_0"]
```

```python
from contextlib import ExitStack

import numpy as np

import concourse.bass as bass
from concourse import mybir

F32 = mybir.dt.float32
F32R = mybir.dt.float32r
ALU = mybir.AluOpType
ACT = mybir.ActivationFunctionType
AX = mybir.AxisListType

B, H, W, C = 8, 256, 256, 64
P = 128
HT = H // P
WF, WH = 2, W // 2
M0 = 12
MR, NR = 17, 17
MX = 2 * (MR - 1)
MODES = MX * NR
NPIX = H * W
G = C // 2
EPS = 1e-5

SLOTS = 8
WS = WH // SLOTS
SLOT = HT * WF * WS * C
WT = 8
TILES = WH // WT
HB = 2 * MR
NE, NO = NR // 2 + 1, NR // 2
CG = 4
GROUPS = C // CG
BANK = 512

CHUNK = 16
CHUNKS = MODES // CHUNK
KG = CHUNK // 4
WIDE = 4
QG = 8
QGROUPS = -(-HB // QG)
PIECES = SLOTS // 2
PW = 2 * WS
ZG = BANK // (WF * PW)
ZGROUPS = C // ZG
FT = SLOTS * HT * WF * 2
PT = FT // PIECES
ZBANKS = (2, 3, 0, 1)
LOW = 64

def columns(names_widths):
    at, out = 0, {}
    for name, width in names_widths:
        out[name] = (at, width)
        at += width
    return out, at


EARLY, EARLY_W = columns([("rows", HT * WF * 2 * HB), ("even", 2 * NE), ("odd", 2 * NO), ("turn", P), ("flip", P),
                          ("flipturn", P), ("minus_j", P), ("place_re", P), ("place_im", P), ("place_conj", P),
                          ("pair", P), ("pair_top", P), ("spread", P), ("ones", 1), ("eps", 1), ("minus_n_top", 1),
                          ("two_top", 1)])
STEPS = ["group_sums", "mean0", "meansq_x", "mean0_sq", "var0", "inv0", "dc0", "staged0", "staged0_dc", "y0_a",
         "y0_b", "yh", "yh_dc", "cross", "cross_yh", "add_dc", "quad", "dquad", "seed_n0", "seed", "mean1",
         "var1_part", "mean1_sq", "var1", "add_modes", "inv1", "inv1n", "add_n0", "add_conj", "dc1"]
AFTER = {name: i + 1 for i, name in enumerate(STEPS)}
LATE, LATE_W = columns([("ident", P)])
BACK, BACK_W = columns([("rows_high", HT * P), ("rows_low", HT * P), ("cols_high", W), ("cols_low", W)])


def rounded(a):
    bits = np.asarray(a, np.float32).view(np.uint32).astype(np.uint64)
    return ((bits + 0x7FF + ((bits >> 12) & 1)) & 0xFFFFF000).astype(np.uint32).view(np.float32).astype(np.float64)


def constants():
    early, late = np.zeros((P, EARLY_W)), np.zeros((P, LATE_W))

    def put(t, where, name, value, row=0):
        a, w = where[name]
        value = value.reshape(value.shape[0], -1)
        t[row:row + value.shape[0], a:a + value.shape[1]] = value

    m, n, h = np.arange(MR), np.arange(NR), np.arange(H)
    angle = 2 * np.pi * ((h[:, None] * m[None, :]) % H) / H
    basis = np.stack([np.cos(angle), np.sin(angle)], -1)
    rows = np.zeros((P, HT, WF, 2, MR, 2))
    for ht in range(HT):
        for wf in range(WF):
            for odd in range(2):
                rows[:, ht, wf, odd] = basis[ht * P:(ht + 1) * P] * (-1 if wf and odd else 1)
    put(early, EARLY, "rows", rows)
    put(early, EARLY, "even", basis[:WH, 0::2].transpose(0, 2, 1))
    put(early, EARLY, "odd", basis[:WH, 1::2].transpose(0, 2, 1))
    eye, none = np.eye(C), np.zeros((C, C))
    blocks = {"turn": [[none, -eye], [eye, none]], "flip": [[eye, none], [none, -eye]],
              "flipturn": [[none, eye], [eye, none]], "minus_j": [[none, eye], [-eye, none]]}
    for name, b in blocks.items():
        put(early, EARLY, name, np.block(b).T)
    put(early, EARLY, "place_re", np.hstack([0.5 * eye, none]))
    put(early, EARLY, "place_im", np.hstack([none, 0.5 * eye]))
    put(early, EARLY, "place_conj", np.hstack([none, -0.5 * eye]))
    pair = np.kron(np.eye(G), np.ones((2, 2))) / (2 * NPIX)
    put(early, EARLY, "pair", np.block([[pair, pair], [pair, pair]]))
    put(early, EARLY, "pair_top", np.block([[pair, pair], [none, none]]))
    put(early, EARLY, "spread", np.tile(np.kron(np.eye(G), np.ones((1, 2))), (1, 2)) / (2 * NPIX))
    put(early, EARLY, "ones", np.ones((P, 1)))
    put(early, EARLY, "eps", np.full((P, 1), EPS))
    top = np.repeat([1.0, 0.0], C)[:, None]
    put(early, EARLY, "minus_n_top", -NPIX * top)
    put(early, EARLY, "two_top", 2 * top)
    put(late, LATE, "ident", np.eye(P))
    back = np.zeros((P, BACK_W))
    weight = np.where(n == 0, 1.0, 2.0)[:, None]
    for name, value in (("rows", basis.transpose(1, 2, 0).reshape(HB, H)),
                        ("cols", (basis.transpose(2, 1, 0) * weight).reshape(2 * NR, W))):
        high = rounded(value)
        for row in (0, LOW):
            put(back, BACK, name + "_high", high, row)
            put(back, BACK, name + "_low", rounded(value - high), row)
    return early.astype(np.float32), late.astype(np.float32), back.astype(np.float32)


def spectral_layers(nc, x, w_re, w_im, k_re, k_im, early_c, late_c, back_c, out):
    ctx = ExitStack()
    with ctx:
        def sem(name):
            return ctx.enter_context(nc.semaphore(name))

        place = [1152]

        def sb(name, width, dtype=F32, at=None):
            here = place[0] if at is None else at
            if at is None:
                place[0] += -(-width * 4 // 32) * 32
            return nc.alloc_sbuf_tensor_at(name, [P, width], dtype, offset=here)

        ring = sb("ring", SLOTS * SLOT)
        xm_at = place[0]
        xm = sb("xm", MODES * B)
        qs = sb("qs", C * HB, F32R, at=xm_at)
        arena_at = place[0]
        arena = sb("arena", MODES * 2 * B + 2 * WF * PW * C)
        z = sb("z", 2 * WF * PW * C, F32R, at=arena_at + MODES * 2 * B * 4)
        early = sb("early", EARLY_W)
        late = sb("late", LATE_W)
        back = sb("back", BACK_W, F32R)
        small = sb("small", 16 * B)
        banks = ctx.enter_context(nc.psum_tensor("banks", [P, 8, BANK], F32))

        def const(name, rows=P):
            t, where = (early, EARLY) if name in EARLY else (late, LATE)
            a, w = where[name]
            return t[0:rows, a:a + w]

        def split(name, a=0, w=None):
            at, width = BACK[name]
            return back[:, at + a:at + a + (w or width)]

        xs = ring[:, :].rearrange("p (s ht wf w c) -> p s ht wf w c", s=SLOTS, ht=HT, wf=WF, w=WS)
        xpos = ring[:, :].rearrange("p (hf pos g two) -> p hf g pos two", hf=2, g=G, two=2)
        xmv = xm[:, :].rearrange("p (m n b) -> p m n b", n=NR, b=B)

        def part(a, w, rows=P):
            return arena[0:rows, a:a + w], a + w

        rows_f, at = part(0, C * WH, 2 * HB)
        rows_t, at = part(at, 2 * HB * C)
        cols_f, at = part(at, 2 * MR * NR)
        bn, at = part(at, 2 * G * 6)
        sqa, at = part(at, 2 * G * 2)
        sqb, at = part(at, 2 * G * 2)
        sumsq, at = part(at, B * G)
        assert at <= arena.shape[1]
        rows_f = rows_f.rearrange("k (c w) -> k c w", c=C)
        rows_tv = rows_t.rearrange("w (k c) -> w k c", c=C)
        cols_fv = cols_f.rearrange("p (q m n) -> p q m n", q=2, m=MR)
        bnv = bn.rearrange("p (hf g six) -> p hf g six", hf=2, g=G)
        bns = bn.rearrange("p (hg eo three) -> p hg eo three", eo=2, three=3)
        back_raw = arena[:, arena.shape[1] - BACK_W:]
        assert at <= arena.shape[1] - BACK_W
        sumsqv = sumsq.rearrange("p (b g) -> p b g", b=B)
        L0 = M0 * M0
        w0, at0 = part(0, C * L0)
        xs0, at0x = part(at0, L0 * 2 * B)
        y0, at1 = part(at0x, L0 * 2 * B, C)
        yh, at1 = part(at1, L0 * B)
        tmp, at1 = part(at1, L0 * B)
        w0v = w0.rearrange("p (o f) -> p o f", f=L0)
        xs0v = xs0.rearrange("p (m n v b) -> p m n v b", m=M0, n=M0, v=2)
        xs0f = xs0.rearrange("p (f v b) -> p f v b", v=2, b=B)
        y0v = y0.rearrange("p (m n vb) -> p m n vb", m=M0, n=M0)
        y0f = y0.rearrange("p (f v b) -> p f v b", v=2, b=B)
        res, atr = part(0, MODES * 2 * B, C)
        assert atr <= at0
        raw, at2 = part(at0, 2 * CHUNK * C)
        assert at2 <= at0x
        raw2, at3 = part(at0x, 2 * CHUNK * C)
        kt, at3 = part(at3, 2 * CHUNK * C)
        assert at3 <= at1
        xst, at3 = part(at1, 2 * CHUNK * 2 * B)
        assert at3 <= arena.shape[1]
        rawv = raw.rearrange("p (k g ri e j) -> p k g ri e j", k=2, g=KG, ri=2, e=2)
        raw2v = raw2.rearrange("p (k g e rj) -> p k g e rj", k=2, g=KG, e=2)
        ktv = kt.rearrange("p (k f i) -> p k f i", k=2, f=CHUNK)
        xstv = xst.rearrange("p (k f v b) -> p k f v b", k=2, f=CHUNK, v=2)
        resv = res.rearrange("p (m n v b) -> p m n v b", n=NR, v=2, b=B)
        resf = res.rearrange("p (f vb) -> p f vb", vb=2 * B)
        tb = early[0:C, 0:HB * 2 * NR].rearrange("o (m r q n) -> o m r q n", m=MR, r=2, q=2)
        tbf = early[0:C, 0:HB * 2 * NR].rearrange("o (k nb) -> o k nb", k=HB)
        qsv = qs[:, :].rearrange("nb (o k) -> nb o k", k=HB)
        zv = z[:, :].rearrange("p (j wf w o) -> p j wf w o", j=2, wf=WF, w=PW)
        zg_view = z[:, :].rearrange("p (j x o) -> p j o x", j=2, o=C)

        def vec(i, rows=P):
            return small[0:rows, i * B:(i + 1) * B]

        gsum, mean0, mean0_sq, var0, std0, inv0, dc0, quad, dquad = (vec(i) for i in range(9))
        mean1, mean1_sq, var1, std1, inv1, inv1n, meansq_x = (vec(i) for i in range(9, 16))

        row_basis_loaded, consts_loaded, back_loaded = sem("row_basis_loaded"), sem("consts_loaded"), sem("back_loaded")
        pads_cleared = sem("pads_cleared")
        x_loaded = [sem(f"x_loaded{s}") for s in range(SLOTS)]
        rows_done, rows_stored = sem("rows_done"), sem("rows_stored")
        turned, turn_stored = sem("turned"), sem("turn_stored")
        cols_done, cols_stored = sem("cols_done"), sem("cols_stored")
        modes_done, modes_stored = sem("modes_done"), sem("modes_stored")
        stats_done, stat_step, sumsq_done = sem("stats_done"), sem("stat_step"), sem("sumsq_done")
        w0_loaded = sem("w0_loaded")
        pe_mix, act_mix, dve_mix = sem("pe_mix"), sem("act_mix"), sem("dve_mix")
        y0_done, y0_stored = sem("y0_done"), sem("y0_stored")
        res_cleared = sem("res_cleared")
        k_loaded = [sem(f"k_loaded{i}") for i in range(2)]
        regrouped_act, regrouped_dve = sem("regrouped_act"), sem("regrouped_dve")
        kt_done, kt_act, kt_dve = sem("kt_done"), sem("kt_act"), sem("kt_dve")
        staged, turned_done, turned_stored = sem("staged"), sem("turned_done"), sem("turned_stored")
        mixed, summed = sem("mixed"), sem("summed")
        split_ready, tb_cleared, tb_minus = sem("split_ready"), sem("tb_cleared"), sem("tb_minus")
        tb_ready, q_done, q_high, q_low = sem("tb_ready"), sem("q_done"), sem("q_high"), sem("q_low")
        z_done, z_high, z_low = sem("z_done"), sem("z_high"), sem("z_low")
        field_done, added = sem("field_done"), sem("added")
        stored = [sem(f"stored{s}") for s in range(SLOTS)]

        x_dram = x.rearrange("b (ht p) (wf s w) c -> b s ht p wf (w c)", p=P, wf=WF, s=SLOTS)
        out_dram = out.rearrange("b (ht p) (wf s w) c -> b s ht p wf (w c)", p=P, wf=WF, s=SLOTS)
        k_dram = [k.rearrange("x y i j -> (x y i j)").rearrange("(k g p ej) -> k p g ej", g=KG, p=P, ej=2 * C)
                  for k in (k_re, k_im)]

        block = ctx.enter_context(nc.Block())

        @block.sync
        def _(sp):
            a = EARLY["rows"][1]
            sp.dma_start(early[:, 0:a], early_c[:, 0:a]).then_inc(row_basis_loaded, 16)

            def load_x(b, s):
                for ht in range(HT):
                    src = x_dram[bass.ds(b, 1), s, ht].rearrange("b p wf n -> p (b wf) n")
                    sp.dma_start(xs[:, s, ht].rearrange("p wf w c -> p wf (w c)"), src).then_inc(x_loaded[s], 16)

            load_x(0, 0)
            load_x(0, 1)
            sp.dma_start(early[:, a:], early_c[:, a:]).then_inc(consts_loaded, 16)
            sp.dma_start(late[:, :], late_c).then_inc(consts_loaded, 16)
            for s in range(2, SLOTS):
                load_x(0, s)
            sp.dma_start(back_raw, back_c).then_inc(back_loaded, 16)
            with sp.Fori(1, B) as b:
                for s in range(SLOTS):
                    sp.wait_ge(rows_done, (b - 1) * TILES + 2 * s + 2)
                    if s % 4 == 0:
                        sp.wait_ge(stats_done, (b - 1) * TILES + 2 * s + 2)
                    load_x(b, s)
            over_rows = C * WH // L0
            for a, e, used, count in ((0, over_rows, turned, B * GROUPS), (over_rows, C, cols_done, B)):
                sp.wait_ge(used, count)
                for rows, w in ((slice(0, C), w_re), (slice(C, P), w_im)):
                    sp.dma_start(w0v[rows, a:e], w.rearrange("c o m n -> c o (m n)")[:, a:e]).then_inc(w0_loaded, 16)

            def load_k(k, i):
                for ri in range(2):
                    src = k_dram[ri][k] if isinstance(k, int) else \
                        k_dram[ri][bass.ds(k, 1)].rearrange("k p g ej -> p (k g) ej")
                    sp.dma_start(rawv[:, i, :, ri].rearrange("p g e j -> p g (e j)"), src).then_inc(k_loaded[i], 16)

            sp.wait_ge(y0_done, 5)
            load_k(0, 0)
            load_k(1, 1)
            with sp.Fori(1, CHUNKS // 2) as kk:
                for i in range(2):
                    sp.wait_ge(regrouped_act, (kk - 1) * 2 + i + 1)
                    sp.wait_ge(regrouped_dve, (kk - 1) * 2 + i + 1)
                    load_k(2 * kk + i, i)

            def write_out(b, s, k):
                for ht in range(HT):
                    sp.wait_ge(added, k * FT + (s * HT + ht + 1) * (FT // SLOTS // HT))
                    dst = out_dram[bass.ds(b, 1), s, ht].rearrange("b p wf n -> p (b wf) n")
                    sp.dma_start(dst, xs[:, s, ht].rearrange("p wf w c -> p wf (w c)")).then_inc(stored[s], 16)

            def image(k, b, again):
                for s in range(SLOTS):
                    write_out(b, s, k)
                    if again and s >= 2:
                        sp.wait_ge(stored[s - 2], k * 32 + 32)
                        load_x(k, s - 2)
                if again:
                    for s in (SLOTS - 2, SLOTS - 1):
                        sp.wait_ge(stored[s], k * 32 + 32)
                        load_x(k, s)

            image(0, B - 1, True)
            with sp.Fori(1, B - 1) as k:
                image(k, k - 1, True)
            image(B - 1, B - 2, False)
            for s in range(SLOTS):
                sp.wait_ge(stored[s], B * 32)

        @block.tensor
        def _(pe):
            row_basis = const("rows").rearrange("p (ht wf k) -> p ht wf k", ht=HT, wf=WF)

            def row_product(b, t, i):
                ht, wf = i // WF, i % WF
                if i == 0:
                    pe.wait_ge(x_loaded[t // 2], b * 32 + 32)
                    if not (isinstance(b, int) and b == 0 and t < 4):
                        pe.wait_ge(rows_stored, b * TILES + t - 3)
                last = nc.tensor.matmul(banks[0:2 * HB, t % 4], row_basis[:, ht, wf],
                                        xs[:, t // 2, ht, wf, (t % 2) * WT:(t % 2 + 1) * WT, :],
                                        start=(i == 0), stop=(i == HT * WF - 1))
                if i == HT * WF - 1:
                    last.then_inc(rows_done, 1)

            def turn_group(b, g, first):
                if g == 0:
                    pe.wait_ge(rows_stored, b * TILES + TILES)
                if not first:
                    pe.wait_ge(turn_stored, b * GROUPS + g - 1)
                    if g < 2:
                        pe.wait_ge(modes_stored, b * 2)
                elif g >= 2:
                    pe.wait_ge(turn_stored, g - 1)
                for j in range(CG):
                    last = nc.tensor.transpose(banks[:, 4 + g % 2, j * 2 * HB:(j + 1) * 2 * HB],
                                               rows_f[:, g * CG + j, :], const("ident")[0:2 * HB, 0:2 * HB])
                last.then_inc(turned, 1)

            def column_mode(b, i, first, wide=False):
                if i == 0:
                    pe.wait_ge(turn_stored, b * GROUPS + GROUPS)
                    if not first:
                        pe.wait_ge(cols_stored, b * 2)
                odd, m = i // MR, i % MR
                name, width = (("even", 2 * NE), ("odd", 2 * NO))[odd]
                streamed = P if wide else width
                last = nc.tensor.matmul(banks[:, 6 + odd, m * width:m * width + streamed],
                                        rows_t[:, i * 2 * C:(i + 1) * 2 * C],
                                        early[:, EARLY[name][0]:EARLY[name][0] + streamed], start=True, stop=True)
                if i == 2 * MR - 1:
                    last.then_inc(cols_done, 1)

            def complex_modes(b):
                pe.wait_ge(cols_stored, b * 2 + 2)
                for minus, mats in ((0, ("ident", "turn")), (1, ("flip", "flipturn"))):
                    for q in range(2):
                        src = cols_fv[:, q, 16:0:-1, :] if minus else cols_fv[:, q, 0:16, :]
                        last = nc.tensor.matmul(banks[:, 4 + minus, 0:MODES // 2], const(mats[q]), src,
                                                start=(q == 0), stop=(q == 1))
                    last.then_inc(modes_done, 1)

            pe.wait_ge(row_basis_loaded, 16)
            for t in range(TILES):
                for i in range(4):
                    row_product(0, t, i)

            def forward(b, first):
                for t in range(4):
                    for i in range(4):
                        row_product(b, t, i)
                        turn_group(b - 1, t * 4 + i, first)
                ahead = 2 * MR - 7 * 4
                for i in range(ahead):
                    column_mode(b - 1, i, first)
                for t in range(4, TILES):
                    for i in range(4):
                        row_product(b, t, i)
                        if t < 11:
                            column_mode(b - 1, ahead + (t - 4) * 4 + i, first)
                    if t == 12:
                        complex_modes(b - 1)

            pe.wait_ge(consts_loaded, 32)
            forward(1, True)
            with pe.Fori(2, B) as b:
                forward(b, False)
            for g in range(GROUPS):
                turn_group(B - 1, g, False)
            for i in range(2 * MR):
                column_mode(B - 1, i, False, wide=True)
            complex_modes(B - 1)

            pe.wait_ge(sumsq_done, B)
            pe.wait_ge(cols_stored, 2 * B)
            for b in range(B):
                last = nc.tensor.matmul(banks[0:G, 6, b:b + 1], sumsqv[:, b, :], const("ones"), start=True, stop=True)
            last.then_inc(pe_mix, 1)
            pe.wait_ge(modes_stored, 2 * B)
            nc.tensor.matmul(banks[:, 7, 0:B], const("pair_top"), xm[:, 0:B], start=True, stop=True)
            pe.wait_ge(dve_mix, AFTER["group_sums"])
            nc.tensor.matmul(banks[:, 7, B:2 * B], const("spread", G), gsum[0:G], start=True, stop=True
                             ).then_inc(pe_mix, 1)
            pe.wait_ge(dve_mix, AFTER["staged0_dc"])
            for t in range(3):
                nc.tensor.matmul(banks[:, t, 0:48 * B], const("minus_j"), xs0f[:, t * 48:(t + 1) * 48, 0, :],
                                 start=True, stop=True).then_inc(pe_mix, 1)
            pe.wait_ge(w0_loaded, 64)
            for t in range(5):
                f0, f1 = t * 32, min(t * 32 + 32, L0)
                pe.wait_ge(act_mix, 2 + (f1 - 1) // 48)
                for f in reversed(range(f0, f1)):
                    a = max(f0, f - WIDE + 1)
                    last = nc.tensor.matmul(banks[0:C, 3 + t, (a - f0) * 2 * B:(f + 1 - f0) * 2 * B], w0v[:, :, f],
                                            xs0f[:, a:f + 1], start=True, stop=True)
                last.then_inc(y0_done, 1)
            pe.wait_ge(y0_stored, 3)
            pe.wait_ge(dve_mix, AFTER["y0_b"])
            for t in range(3):
                for v, name in enumerate(("place_re", "place_im")):
                    nc.tensor.matmul(banks[:, t, 0:48 * B], const(name, C), y0f[:, t * 48:(t + 1) * 48, v, :],
                                     start=(v == 0), stop=(v == 1))
            for v, name in enumerate(("place_re", "place_conj")):
                last = nc.tensor.matmul(banks[:, 3, 0:(M0 - 1) * B], const(name, C),
                                        y0v[:, M0 - 1:0:-1, 0, v * B:(v + 1) * B], start=(v == 0), stop=(v == 1))
            last.then_inc(pe_mix, 1)
            pe.wait_ge(dve_mix, AFTER["dquad"])
            nc.tensor.matmul(banks[:, 4, 0:B], const("pair_top"), xm[:, 0:B], start=True, stop=True)
            nc.tensor.matmul(banks[:, 4, B:2 * B], const("pair"), dquad, start=True, stop=True).then_inc(pe_mix, 1)

            def prepare(k, i, reused):
                pe.wait_ge(regrouped_act, k + 1)
                pe.wait_ge(regrouped_dve, k + 1)
                if reused:
                    pe.wait_ge(kt_act, k - 1)
                    pe.wait_ge(kt_dve, k - 1)
                for e in range(2):
                    for g in range(KG):
                        last = nc.tensor.transpose(banks[:, 2 * i + e, g * P:(g + 1) * P], raw2v[:, i, g, e, :],
                                                   const("ident"))
                    last.then_inc(kt_done, 1)
                pe.wait_ge(staged, k + 1)
                if reused:
                    pe.wait_ge(turned_stored, k - 1)
                nc.tensor.matmul(banks[:, 4 + i, 0:CHUNK * B], const("minus_j"), xstv[:, i, :, 0, :],
                                 start=True, stop=True).then_inc(turned_done, 1)

            def mix(k, i, reused):
                pe.wait_ge(kt_act, k + 1)
                pe.wait_ge(kt_dve, k + 1)
                pe.wait_ge(turned_stored, k + 1)
                if reused:
                    pe.wait_ge(summed, k - 1)
                for f in reversed(range(CHUNK)):
                    a = max(0, f - WIDE + 1)
                    last = nc.tensor.matmul(banks[0:C, 6 + i, a * 2 * B:(f + 1) * 2 * B], ktv[:, i, f],
                                            xstv[:, i, a:f + 1], start=True, stop=True)
                last.then_inc(mixed, 1)

            prepare(0, 0, False)
            prepare(1, 1, False)
            mix(0, 0, False)
            prepare(2, 0, True)
            mix(1, 1, False)
            with pe.Fori(1, CHUNKS // 2 - 1) as kk:
                prepare(2 * kk + 1, 1, True)
                mix(2 * kk, 0, True)
                prepare(2 * kk + 2, 0, True)
                mix(2 * kk + 1, 1, True)
            prepare(CHUNKS - 1, 1, True)
            mix(CHUNKS - 2, 0, True)
            mix(CHUNKS - 1, 1, True)

            def turn_basis(k, j, first=False):
                if j == 0:
                    pe.wait_ge(tb_ready, k + 1)
                if j >= 4:
                    pe.wait_ge(q_low, k * QGROUPS + j - 3)
                a = j * QG * 2 * NR
                last = nc.tensor.matmul(banks[:, j % 4, 0:C], early[0:C, a:a + P], const("ident")[0:C, 0:C],
                                        start=True, stop=True)
                for c in range(1, min(QG, HB - j * QG)):
                    last = nc.tensor.transpose(banks[0:2 * NR, j % 4, c * C:(c + 1) * C], tbf[:, j * QG + c, :],
                                               const("ident")[0:C, 0:C])
                last.then_inc(q_done, 1)

            def columns_group(k, n, first=False):
                j, zg = n // ZGROUPS, n % ZGROUPS
                if n == 0:
                    pe.wait_ge(q_low, k * QGROUPS + QGROUPS)
                if first and n == 0:
                    pe.wait_ge(pads_cleared, 1)
                    pe.wait_ge(split_ready, 1)
                if not (first and n < 4):
                    pe.wait_ge(z_low, k * PIECES * ZGROUPS + n - 3)
                for c in range(ZG):
                    for part in ("high", "low"):
                        where = split("cols_" + part).rearrange("nb (wf w) -> nb wf w", wf=WF)
                        last = nc.tensor.matmul(banks[0:HB, ZBANKS[n % 4], c * WF * PW:(c + 1) * WF * PW],
                                                qsv[:, zg * ZG + c, :], where[:, :, j * PW:(j + 1) * PW],
                                                start=(part == "high"), stop=(part == "low"))
                last.then_inc(z_done, 1)

            def rows_tile(k, t, first=False):
                j, s, ht, wf, wh = t // PT, t // 8, t // 4 % 2, t // 2 % 2, t % 2
                if t % PT == 0:
                    pe.wait_ge(z_low, k * PIECES * ZGROUPS + (j + 1) * ZGROUPS)
                if first and t % PT == 0 and j < 2:
                    pe.wait_ge(pads_cleared, 2 + j)
                if not (first and t < 4):
                    pe.wait_ge(added, k * FT + t - 3)
                w_at = s % 2 * WS + wh * WT
                for part in ("high", "low"):
                    last = nc.tensor.matmul(banks[:, 4 + t % 4, :], split("rows_" + part, ht * P, P),
                                            zv[:, j % 2, wf, w_at:w_at + WT, :],
                                            start=(part == "high"), stop=(part == "low"))
                last.then_inc(field_done, 1)

            def inverse(k, first, more):
                for t in range(FT):
                    j, i = t // PT, t % PT
                    rows_tile(k, t, first)
                    if j + 1 < PIECES:
                        if i % 2 == 1:
                            columns_group(k, (j + 1) * ZGROUPS + i // 2, first)
                    elif more:
                        if i < QGROUPS:
                            turn_basis(k + 1, i)
                        elif PT - 1 - ZGROUPS <= i < PT - 1:
                            columns_group(k + 1, i - (PT - 1 - ZGROUPS))

            for j in range(QGROUPS):
                turn_basis(0, j, True)
            for n in range(ZGROUPS):
                columns_group(0, n, True)
            inverse(0, True, True)
            with pe.Fori(1, B - 1) as k:
                inverse(k, False, True)
            inverse(B - 1, False, False)

        @block.scalar
        def _(act):
            def store_rows(b, t, reused):
                act.wait_ge(rows_done, b * TILES + t + 1)
                if reused and t == 0:
                    act.wait_ge(turned, b * GROUPS)
                nc.scalar.copy(rows_f[:, :, t * WT:(t + 1) * WT].rearrange("k c w -> k w c"),
                               banks[0:2 * HB, t % 4, :].rearrange("k (w c) -> k w c", c=C)).then_inc(rows_stored, 1)

            def store_turned(b, g, reused):
                act.wait_ge(turned, b * GROUPS + g + 1)
                if reused and g == 0:
                    act.wait_ge(cols_done, b)
                nc.scalar.copy(rows_tv[:, :, g * CG:(g + 1) * CG].rearrange("w k c -> w c k"),
                               banks[:, 4 + g % 2, 0:CG * 2 * HB].rearrange("w (c k) -> w c k", c=CG)
                               ).then_inc(turn_stored, 1)

            def store_columns(b, reused):
                act.wait_ge(cols_done, b + 1)
                if reused:
                    act.wait_ge(modes_done, 2 * b)
                for odd, n in ((0, NE), (1, NO)):
                    nc.scalar.copy(cols_fv[:, :, :, odd::2].rearrange("p q m n -> p m q n"),
                                   banks[:, 6 + odd, 0:MR * 2 * n].rearrange("p (m q n) -> p m q n", m=MR, q=2)
                                   ).then_inc(cols_stored, 1)

            def store_modes(b):
                act.wait_ge(modes_done, 2 * b + 2)
                for minus in range(2):
                    dst = xm[:, :].rearrange("p (f b) -> p f b", b=B)[:, minus * MODES // 2:(minus + 1) * MODES // 2,
                                                                     bass.ds(b, 1)]
                    nc.scalar.copy(dst, banks[:, 4 + minus, 0:MODES // 2].rearrange("p (f b) -> p f b", b=1)
                                   ).then_inc(modes_stored, 1)

            for t in range(TILES):
                store_rows(0, t, False)
            act.wait_ge(back_loaded, 16)
            nc.scalar.copy(back[:, :], back_raw).then_inc(split_ready, 1)

            def forward(b, first):
                for g in range(GROUPS):
                    store_turned(b - 1, g, not first)
                for t in range(11):
                    store_rows(b, t, True)
                store_columns(b - 1, not first)
                for t in range(11, 13):
                    store_rows(b, t, True)
                store_modes(b - 1)
                for t in range(13, TILES):
                    store_rows(b, t, True)

            forward(1, True)
            with act.Fori(2, B) as b:
                forward(b, False)
            for g in range(GROUPS):
                store_turned(B - 1, g, True)
            store_columns(B - 1, True)
            store_modes(B - 1)

            act.wait_ge(dve_mix, AFTER["var0"])
            nc.scalar.activation(std0, var0, ACT.Sqrt, bias=const("eps")).then_inc(act_mix, 1)
            for t in range(3):
                act.wait_ge(pe_mix, 3 + t)
                nc.scalar.copy(xs0f[:, t * 48:(t + 1) * 48, 1, :],
                               banks[:, t, 0:48 * B].rearrange("p (f b) -> p f b", b=B)).then_inc(act_mix, 1)
            for t, n in ((0, 32), (2, 32), (4, 16)):
                act.wait_ge(y0_done, t + 1)
                nc.scalar.copy(y0[:, t * BANK:t * BANK + n * 2 * B], banks[0:C, 3 + t, 0:n * 2 * B]
                               ).then_inc(y0_stored, 1)
            def regroup(k, i, loads, reused):
                act.wait_ge(k_loaded[i], loads * 32)
                if reused:
                    act.wait_ge(kt_done, 2 * k - 2)
                nc.scalar.copy(raw2v[:, i, :, :, 0:C], rawv[:, i, :, 0]).then_inc(regrouped_act, 1)

            def prepare(k, i, reused):
                act.wait_ge(kt_done, 2 * k + 1)
                if reused:
                    act.wait_ge(mixed, k - 1)
                nc.scalar.copy(ktv[:, i, :, 0::2], banks[:, 2 * i, :].rearrange("p (f i) -> p f i", f=CHUNK)
                               ).then_inc(kt_act, 1)
                act.wait_ge(turned_done, k + 1)
                nc.scalar.copy(xstv[:, i, :, 1, :], banks[:, 4 + i, 0:CHUNK * B].rearrange("p (f b) -> p f b", b=B)
                               ).then_inc(turned_stored, 1)

            act.wait_ge(pe_mix, 6)
            act.wait_ge(dve_mix, AFTER["seed"])
            regroup(0, 0, 1, False)
            act.wait_ge(dve_mix, AFTER["var1"])
            nc.scalar.activation(std1, var1, ACT.Sqrt, bias=const("eps")).then_inc(act_mix, 1)
            regroup(1, 1, 1, False)
            act.wait_ge(dve_mix, AFTER["add_n0"])
            prepare(0, 0, False)
            regroup(2, 0, 2, True)
            prepare(1, 1, False)
            with act.Fori(1, CHUNKS // 2 - 1) as kk:
                regroup(2 * kk + 1, 1, kk + 1, True)
                prepare(2 * kk, 0, True)
                regroup(2 * kk + 2, 0, kk + 2, True)
                prepare(2 * kk + 1, 1, True)
            regroup(CHUNKS - 1, 1, CHUNKS // 2, True)
            prepare(CHUNKS - 2, 0, True)
            prepare(CHUNKS - 1, 1, True)

            def turned_high(k, j):
                n = min(QG, HB - j * QG)
                act.wait_ge(q_done, k * QGROUPS + j + 1)
                nc.scalar.copy(qsv[0:2 * NR, :, j * QG:j * QG + n].rearrange("nb o k -> nb k o"),
                               banks[0:2 * NR, j % 4, 0:n * C].rearrange("nb (k o) -> nb k o", o=C)
                               ).then_inc(q_high, 1)

            def columns_high(k, n):
                j, zg = n // ZGROUPS, n % ZGROUPS
                act.wait_ge(z_done, k * PIECES * ZGROUPS + n + 1)
                nc.scalar.copy(zg_view[0:HB, j % 2, zg * ZG:(zg + 1) * ZG, :],
                               banks[0:HB, ZBANKS[n % 4], :].rearrange("p (o x) -> p o x", o=ZG)).then_inc(z_high, 1)

            def inverse(k, more):
                for n in range(ZGROUPS, PIECES * ZGROUPS):
                    columns_high(k, n)
                if more:
                    for j in range(QGROUPS):
                        turned_high(k + 1, j)
                    for n in range(ZGROUPS):
                        columns_high(k + 1, n)

            act.wait_ge(pads_cleared, 1)
            for j in range(QGROUPS):
                turned_high(0, j)
            act.wait_ge(pads_cleared, 2)
            for n in range(ZGROUPS):
                columns_high(0, n)
            act.wait_ge(pads_cleared, 3)
            inverse(0, True)
            with act.Fori(1, B - 1) as k:
                inverse(k, True)
            inverse(B - 1, False)

        @block.gpsimd
        def _(pool):
            pool.wait_ge(y0_done, 5)
            nc.gpsimd.memset(res, 0.0).then_inc(res_cleared, 1)
            pool.wait_ge(staged, CHUNKS)
            nc.gpsimd.memset(qs[:, :].bitcast(F32), 0.0).then_inc(pads_cleared, 1)
            pool.wait_ge(mixed, CHUNKS)
            for j in range(2):
                half = z[:, j * WF * PW * C:(j + 1) * WF * PW * C]
                nc.gpsimd.memset(half.bitcast(F32), 0.0).then_inc(pads_cleared, 1)

        @block.vector
        def _(dve):
            def statistics(b):
                for hf in range(2):
                    for s in range(4 * hf, 4 * hf + 4):
                        dve.wait_ge(x_loaded[s], b * 32 + 32)
                    for g in range(G):
                        last = nc.vector.bn_stats(bnv[:, hf, g, :], xpos[:, hf, g])
                    last.then_inc(stats_done, TILES // 2)
                dve.wait_ge(stats_done, b * TILES + TILES)
                nc.vector.tensor_tensor(sqa.rearrange("p (x y) -> p x y", y=2), bns[:, :, :, 1], bns[:, :, :, 1],
                                        ALU.mult).then_inc(stat_step, 1)
                dve.wait_ge(stat_step, 2 * b + 1)
                nc.vector.scalar_tensor_tensor(sqb.rearrange("p (x y) -> p x y", y=2),
                                               sqa.rearrange("p (x y) -> p x y", y=2), float(SLOTS // 2 * SLOT // C),
                                               bns[:, :, :, 2], ALU.mult, ALU.add).then_inc(stat_step, 1)
                dve.wait_ge(stat_step, 2 * b + 2)
                nc.vector.tensor_reduce(sumsqv[:, bass.ds(b, 1), :].rearrange("p b g -> p (b g)"),
                                        sqb.rearrange("p (hf g eo) -> p g hf eo", hf=2, g=G), AX.XY,
                                        ALU.add).then_inc(sumsq_done, 1)

            with dve.Fori(0, B) as b:
                statistics(b)

            done = [0]

            def step(name, ins):
                done[0] += 1
                assert AFTER[name] == done[0]
                ins.then_inc(dve_mix, 1)

            def after(name):
                dve.wait_ge(dve_mix, AFTER[name])

            v = nc.vector

            def regroup(k, i, loads, reused):
                dve.wait_ge(k_loaded[i], loads * 32)
                if reused:
                    dve.wait_ge(kt_done, 2 * k - 2)
                v.tensor_copy(raw2v[:, i, :, :, C:2 * C], rawv[:, i, :, 1]).then_inc(regrouped_dve, 1)

            dve.wait_ge(pe_mix, 1)
            step("group_sums", v.tensor_copy(gsum[0:G], banks[0:G, 6, 0:B]))
            dve.wait_ge(pe_mix, 2)
            step("mean0", v.tensor_copy(mean0, banks[:, 7, 0:B]))
            step("meansq_x", v.tensor_copy(meansq_x, banks[:, 7, B:2 * B]))
            after("meansq_x")
            step("mean0_sq", v.tensor_tensor(mean0_sq, mean0, mean0, ALU.mult))
            after("mean0_sq")
            step("var0", v.tensor_tensor(var0, meansq_x, mean0_sq, ALU.subtract))
            dve.wait_ge(act_mix, 1)
            step("inv0", v.reciprocal(inv0, std0))
            dve.wait_ge(modes_stored, 2 * B)
            step("dc0", v.scalar_tensor_tensor(dc0, mean0, const("minus_n_top"), xm[:, 0:B], ALU.mult, ALU.add))
            after("dc0")
            step("staged0", v.tensor_tensor(xs0v[:, :, :, 0, :], xmv[:, 0:M0, 0:M0, :],
                                            inv0.rearrange("p (m n b) -> p m n b", m=1, n=1
                                                           ).broadcast_to([P, M0, M0, B]), ALU.mult))
            after("staged0")
            step("staged0_dc", v.tensor_tensor(xs0[:, 0:B], dc0, inv0, ALU.mult))
            for t, name in ((1, "y0_a"), (3, "y0_b")):
                dve.wait_ge(y0_done, t + 1)
                step(name, v.tensor_copy(y0[:, t * BANK:(t + 1) * BANK], banks[0:C, 3 + t, :]))
            dve.wait_ge(pe_mix, 6)
            step("yh", v.tensor_copy(yh.rearrange("p (t f) -> p t f", t=3), banks[:, 0:3, 0:48 * B]))
            after("yh")
            step("yh_dc", v.tensor_scalar(yh[:, 0:B], banks[:, 0, 0:B], const("two_top"), None, ALU.mult))
            after("yh_dc")
            xsel = xmv[:, 0:M0, 0:M0, :].rearrange("p m n b -> p m (n b)")
            yhm = yh.rearrange("p (m nb) -> p m nb", m=M0)
            step("cross", v.scalar_tensor_tensor(tmp.rearrange("p (m nb) -> p m nb", m=M0), xsel, 2.0, yhm,
                                                 ALU.mult, ALU.add))
            after("cross")
            step("cross_yh", v.tensor_tensor(tmp, tmp, yh, ALU.mult))
            step("add_dc", v.tensor_tensor(xm[:, 0:B], xm[:, 0:B], yh[:, 0:B], ALU.add))
            after("add_dc")
            step("quad", v.tensor_reduce(quad, tmp.rearrange("p (f b) -> p b f", b=B), AX.X, ALU.add))
            after("quad")
            step("dquad", v.scalar_tensor_tensor(dquad, quad, 2.0, tmp[:, 0:B], ALU.mult, ALU.subtract))
            dve.wait_ge(y0_stored, 3)
            dve.wait_ge(res_cleared, 1)
            resm = res.rearrange("p (m n vb) -> p m n vb", m=MX, n=NR)
            step("seed_n0", v.tensor_scalar(resm[:, 0:M0, 0, :], y0v[:, :, 0, :], 1.0 / NPIX, None, ALU.mult))
            step("seed", v.tensor_scalar(resm[:, 0:M0, 1:M0, :], y0v[:, :, 1:M0, :], 0.5 / NPIX, None, ALU.mult))
            after("seed")
            regroup(0, 0, 1, False)
            dve.wait_ge(pe_mix, 7)
            step("mean1", v.tensor_copy(mean1, banks[:, 4, 0:B]))
            step("var1_part", v.scalar_tensor_tensor(inv1, banks[:, 4, B:2 * B], 1.0 / NPIX, meansq_x, ALU.mult,
                                                     ALU.add))
            after("var1_part")
            step("mean1_sq", v.tensor_tensor(mean1_sq, mean1, mean1, ALU.mult))
            after("mean1_sq")
            step("var1", v.tensor_tensor(var1, inv1, mean1_sq, ALU.subtract))
            regroup(1, 1, 1, False)
            step("add_modes", v.tensor_tensor(xmv[:, 0:M0, 1:M0, :], xmv[:, 0:M0, 1:M0, :],
                                              yhm[:, :, B:].rearrange("p m (n b) -> p m n b", b=B), ALU.add))
            dve.wait_ge(act_mix, 5)
            step("inv1", v.reciprocal(inv1, std1))
            after("inv1")
            step("inv1n", v.tensor_scalar(inv1n, inv1, 1.0 / NPIX, None, ALU.mult))
            step("add_n0", v.tensor_tensor(xmv[:, 1:M0, 0, :], xmv[:, 1:M0, 0, :], yhm[:, 1:, 0:B], ALU.add))
            step("add_conj", v.tensor_tensor(xmv[:, MX - M0 + 1:MX, 0, :], xmv[:, MX - M0 + 1:MX, 0, :],
                                             banks[:, 3, 0:(M0 - 1) * B].rearrange("p (m b) -> p m b", b=B), ALU.add))
            step("dc1", v.scalar_tensor_tensor(xm[:, 0:B], mean1, const("minus_n_top"), xm[:, 0:B], ALU.mult,
                                               ALU.add))
            after("dc1")

            xf = xm[:, :].rearrange("p (f b) -> p f b", b=B)

            def stage(k, i, reused):
                if reused:
                    dve.wait_ge(mixed, k - 1)
                v.tensor_tensor(xstv[:, i, :, 0, :], xf[:, bass.ds(k * CHUNK, CHUNK), :],
                                inv1n.rearrange("p (f b) -> p f b", f=1).broadcast_to([P, CHUNK, B]), ALU.mult
                                ).then_inc(staged, 1)

            def store_kernels(k, i):
                dve.wait_ge(kt_done, 2 * k + 2)
                v.tensor_copy(ktv[:, i, :, 1::2], banks[:, 2 * i + 1, :].rearrange("p (f i) -> p f i", f=CHUNK)
                              ).then_inc(kt_dve, 1)

            def add_up(k, i):
                dve.wait_ge(mixed, k + 1)
                dst = resf[:, bass.ds(k * CHUNK, CHUNK), :]
                v.tensor_tensor(dst, dst, banks[0:C, 6 + i, 0:CHUNK * 2 * B].rearrange("p (f vb) -> p f vb", f=CHUNK),
                                ALU.add).then_inc(summed, 1)

            stage(0, 0, False)
            store_kernels(0, 0)
            stage(1, 1, False)
            regroup(2, 0, 2, True)
            store_kernels(1, 1)
            stage(2, 0, True)
            add_up(0, 0)
            regroup(3, 1, 2, True)
            store_kernels(2, 0)
            with dve.Fori(1, CHUNKS // 2 - 1) as kk:
                stage(2 * kk + 1, 1, True)
                add_up(2 * kk - 1, 1)
                regroup(2 * kk + 2, 0, kk + 2, True)
                store_kernels(2 * kk + 1, 1)
                stage(2 * kk + 2, 0, True)
                add_up(2 * kk, 0)
                regroup(2 * kk + 3, 1, kk + 2, True)
                store_kernels(2 * kk + 2, 0)
            stage(CHUNKS - 1, 1, True)
            add_up(CHUNKS - 3, 1)
            store_kernels(CHUNKS - 1, 1)
            add_up(CHUNKS - 2, 0)
            add_up(CHUNKS - 1, 1)
            dve.wait_ge(summed, CHUNKS)

            v.memset(tb[:, 0, 1], 0.0).then_inc(tb_cleared, 1)
            dve.wait_ge(tb_cleared, 1)

            def bases(k, b):
                plus = resv[:, 1:MR - 1, :, :, bass.ds(b, 1)].rearrange("o m n v b -> o m v (n b)")
                minus = resv[:, MR:MX, :, :, bass.ds(b, 1)].rearrange("o m n v b -> o m v (n b)")
                edge = resv[:, 0:MR:MR - 1, :, :, bass.ds(b, 1)].rearrange("o m n v b -> o m v (n b)")
                inner, back = tb[:, 1:MR - 1], tb[:, MR - 2:0:-1]
                v.tensor_copy(back[:, :, 0], minus)
                v.tensor_scalar(back[:, :, 1, 0], minus[:, :, 1], -1.0, None, ALU.mult)
                v.tensor_copy(back[:, :, 1, 1], minus[:, :, 0]).then_inc(tb_minus, 1)
                v.tensor_copy(tb[:, 0:MR:MR - 1, 0], edge)
                v.tensor_scalar(tb[:, MR - 1, 1, 0], edge[:, 1, 1], -1.0, None, ALU.mult)
                v.tensor_copy(tb[:, MR - 1, 1, 1], edge[:, 1, 0])
                dve.wait_ge(tb_minus, k + 1)
                v.tensor_tensor(inner[:, :, 0], inner[:, :, 0], plus, ALU.add)
                v.tensor_tensor(inner[:, :, 1, 0], inner[:, :, 1, 0], plus[:, :, 1], ALU.add)
                v.tensor_tensor(inner[:, :, 1, 1], inner[:, :, 1, 1], plus[:, :, 0], ALU.subtract
                                ).then_inc(tb_ready, 1)

            def turned_low(k, j):
                n = min(QG, HB - j * QG)
                dve.wait_ge(q_high, k * QGROUPS + j + 1)
                part = qsv[:, :, j * QG:j * QG + n].rearrange("nb o k -> nb k o")
                v.tensor_tensor(part[LOW:LOW + 2 * NR], banks[0:2 * NR, j % 4, 0:n * C].rearrange(
                    "nb (k o) -> nb k o", o=C), part[0:2 * NR].bitcast(F32), ALU.subtract).then_inc(q_low, 1)

            def columns_low(k, n):
                j, zg = n // ZGROUPS, n % ZGROUPS
                dve.wait_ge(z_high, k * PIECES * ZGROUPS + n + 1)
                part = zg_view[:, j % 2, zg * ZG:(zg + 1) * ZG, :]
                v.tensor_tensor(part[LOW:LOW + HB], banks[0:HB, ZBANKS[n % 4], :].rearrange("p (o x) -> p o x", o=ZG),
                                part[0:HB].bitcast(F32), ALU.subtract).then_inc(z_low, 1)

            def add_field(k, t):
                s, ht, wf, wh = t // 8, t // 4 % 2, t // 2 % 2, t % 2
                if t % 8 == 0:
                    dve.wait_ge(x_loaded[s], k * 32 + B * 32)
                dve.wait_ge(field_done, k * FT + t + 1)
                dst = xs[:, s, ht, wf, wh * WT:(wh + 1) * WT, :]
                v.tensor_tensor(dst, dst, banks[:, 4 + t % 4, :].rearrange("p (w c) -> p w c", c=C), ALU.add
                                ).then_inc(added, 1)

            def image(k, more):
                for t in range(FT):
                    j, i = t // PT, t % PT
                    if more and t == PT:
                        dve.wait_ge(q_done, k * QGROUPS + QGROUPS)
                        bases(k + 1, k)
                    add_field(k, t)
                    if j + 1 < PIECES:
                        if i % 2 == 1 and i >= 3:
                            columns_low(k, (j + 1) * ZGROUPS + i // 2 - 1)
                        if i == PT - 1:
                            columns_low(k, (j + 1) * ZGROUPS + ZGROUPS - 1)
                    elif more:
                        if 1 <= i <= QGROUPS:
                            turned_low(k + 1, i - 1)
                        elif i >= PT - ZGROUPS:
                            columns_low(k + 1, i - (PT - ZGROUPS))

            bases(0, B - 1)
            for j in range(QGROUPS):
                turned_low(0, j)
            for n in range(ZGROUPS):
                columns_low(0, n)
            image(0, True)
            with dve.Fori(1, B - 1) as k:
                image(k, True)
            image(B - 1, False)


_INS = ["x", "L0_conv_w_real", "L0_conv_w_imag", "L1_conv_kernel_re", "L1_conv_kernel_im"]


def kernel(**inputs):
    import numpy as _np
    import concourse.bacc as _bacc
    from concourse import mybir as _mybir
    from concourse.bass_utils import run_bass_kernel_spmd as _run

    nc = _bacc.Bacc("TRN2", target_bir_lowering=False, num_devices=1, dynamic_dma_scratch_size=1024)
    early_c, late_c, back_c = constants()
    arrays = {name: _np.ascontiguousarray(inputs[name]) for name in _INS}
    arrays["early_c"], arrays["late_c"], arrays["back_c"] = early_c, late_c, back_c
    args = [nc.dram_tensor(f"in_{n}", a.shape, _mybir.dt.from_np(a.dtype), kind="ExternalInput").ap()
            for n, a in arrays.items()]
    out = nc.dram_tensor("out_0", (B, H, W, C), _mybir.dt.float32, kind="ExternalOutput").ap()
    spectral_layers(nc, *args, out)
    r = _run(nc, [{f"in_{n}": a for n, a in arrays.items()}], core_ids=[0])
    return r.results[0]["out_0"]
```
